# Optimizing a Trainium2 kernel written in Bass

```python
import numpy as np
import jax
import jax.numpy as jnp

def _softmax(x, axis=-1):
    return jax.nn.softmax(x, axis=axis)

def _gelu(x):
    return jax.nn.gelu(x, approximate=True)

def _silu(x):
    return jax.nn.silu(x)

def _sigmoid(x):
    return jax.nn.sigmoid(x)

def _layernorm(x, axis=-1, eps=1e-05):
    m = jnp.mean(x, axis=axis, keepdims=True)
    v = jnp.var(x, axis=axis, keepdims=True)
    return (x - m) / jnp.sqrt(v + eps)

def _scatter_add(tgt, idx, src, axis=0):
    return tgt.at[idx].add(src)

def _segment_sum(src, seg, n):
    return jax.ops.segment_sum(src, seg, n)
kernel_name = 'mk_prb_d4_jaxref_r8_71c655'

def setup_inputs(seed: int=0):
    np.random.seed(seed)
    _w = jnp.asarray

    def _L0_attn_setup():
        import jax, jax.numpy as jnp
        import numpy as np
        CHUNK = 64
        LR = 0.001

        def _fast_weight(xc, a0, a1, a2):
            h = jax.nn.silu(jnp.einsum('bch,hf->bcf', xc, a0)) * jnp.einsum('bch,hf->bcf', xc, a2)
            return jnp.einsum('bcf,fh->bch', h, a1)

        def _reference_tuple_inner(x, w0, w1, w2):
            B, S, H = x.shape
            nC = S // CHUNK
            xc = x.reshape(B, nC, CHUNK, H).transpose(1, 0, 2, 3)

            def step(carry, x_chunk):
                a0, a1, a2, acc_loss = carry
                out = _fast_weight(x_chunk, a0, a1, a2)
                chunk_loss = jnp.mean((out - x_chunk) ** 2)
                decay = 1.0 - LR * chunk_loss
                return ((a0 * decay, a1 * decay, a2 * decay, acc_loss + chunk_loss), out)
            init = (w0, w1, w2, jnp.float32(0.0))
            (_, _, _, total_loss), outs = jax.lax.scan(step, init, xc)
            output = outs.transpose(1, 0, 2, 3).reshape(B, S, H)
            return (output, total_loss / nC)
        key = jax.random.key(seed)
        k1, k2, k3, k4 = jax.random.split(key, 4)
        B, S, H, F = (4, 512, 128, 512)
        x = jax.random.normal(k1, (B, S, H), dtype=jnp.float32)
        w0 = jax.random.normal(k2, (H, F), dtype=jnp.float32) * 0.02
        w1 = jax.random.normal(k3, (F, H), dtype=jnp.float32) * 0.02
        w2 = jax.random.normal(k4, (H, F), dtype=jnp.float32) * 0.02
        return {'x': x, 'w0': w0, 'w1': w1, 'w2': w2}
    _L0_attn_in = _L0_attn_setup()

    def _L0_ffn_setup():
        import jax, jax.numpy as jnp
        import numpy as np
        N_HEADS = 4
        key = jax.random.key(seed)
        k1, k2, k3, k4 = jax.random.split(key, 4)
        dmodel, n_experts, expert_size = (128, 64, 128)
        B, S = (4, 256)
        x = jax.random.normal(k1, (B, S, dmodel), dtype=jnp.float32)
        expert_sel = jax.random.normal(k2, (n_experts, dmodel), dtype=jnp.float32) * dmodel ** (-0.5)
        keys = jax.random.normal(k3, (n_experts, dmodel, expert_size), dtype=jnp.float32) * dmodel ** (-0.5)
        values = jax.random.normal(k4, (n_experts, expert_size, dmodel), dtype=jnp.float32) * (n_experts * expert_size) ** (-0.5)
        return {'x': x, 'expert_sel': expert_sel, 'keys': keys, 'values': values}
    _L0_ffn_in = _L0_ffn_setup()

    def _L1_attn_setup():
        import jax, jax.numpy as jnp
        import numpy as np
        DIM = 128
        NUM_HEAD = 16
        DIM_HEAD = DIM // NUM_HEAD
        RMS_EPS = 1.1920929e-07
        EPS_LIN = 1e-06
        THETA = 10000.0

        def rmsnorm(x, g, eps=RMS_EPS):
            return x * jax.lax.rsqrt(jnp.mean(x * x, axis=-1, keepdims=True) + eps) * g

        def rope_cos_sin(seq_len, dim_head, dtype=jnp.float32):
            inv_freq = 1.0 / THETA ** (jnp.arange(0, dim_head, 2, dtype=dtype) / dim_head)
            t = jnp.arange(seq_len, dtype=dtype)
            freqs = jnp.outer(t, inv_freq)
            return (jnp.cos(freqs), jnp.sin(freqs))

        def apply_rope(t, cos, sin):
            tr = t[..., 0::2]
            ti = t[..., 1::2]
            out_r = tr * cos - ti * sin
            out_i = tr * sin + ti * cos
            return jnp.stack([out_r, out_i], axis=-1).reshape(t.shape)
        key = jax.random.key(seed)
        ks = jax.random.split(key, 5)
        B, L = (4, 512)
        x = jax.random.normal(ks[0], (B, L, DIM), dtype=jnp.float32)
        Wqkv = jax.random.normal(ks[1], (3 * DIM, DIM), dtype=jnp.float32) * 0.02
        bqkv = jax.random.normal(ks[2], (3 * DIM,), dtype=jnp.float32) * 0.02
        gq = jnp.ones((DIM,), dtype=jnp.float32)
        gk = jnp.ones((DIM,), dtype=jnp.float32)
        Wout = jax.random.normal(ks[3], (DIM, DIM), dtype=jnp.float32) * 0.02
        bout = jax.random.normal(ks[4], (DIM,), dtype=jnp.float32) * 0.02
        gout = jnp.ones((DIM,), dtype=jnp.float32)
        return {'x': x, 'Wqkv': Wqkv, 'bqkv': bqkv, 'gq': gq, 'gk': gk, 'Wout': Wout, 'bout': bout, 'gout': gout}
    _L1_attn_in = _L1_attn_setup()

    def _L1_ffn_setup():
        import jax, jax.numpy as jnp
        import numpy as np
        DIM = 128

        def _reference_tuple_inner(x, W_r, W_k, W_v, mu_r, mu_k):
            B, T, C = x.shape
            x_prev = jnp.concatenate([jnp.zeros((B, 1, C), x.dtype), x[:, :-1, :]], axis=1)
            xr = mu_r * x + (1.0 - mu_r) * x_prev
            xk = mu_k * x + (1.0 - mu_k) * x_prev
            r = jax.nn.sigmoid(jnp.einsum('btc,dc->btd', xr, W_r))
            k = jnp.einsum('btc,dc->btd', xk, W_k)
            k_act = jnp.square(jax.nn.relu(k))
            out = r * jnp.einsum('btc,dc->btd', k_act, W_v)
            new_state = x[:, -1, :]
            return (out, new_state)
        key = jax.random.key(seed)
        ks = jax.random.split(key, 6)
        B, T, C = (8, 256, DIM)
        x = jax.random.normal(ks[0], (B, T, C), dtype=jnp.float32)
        s = 1.0 / np.sqrt(C)
        W_r = jax.random.uniform(ks[1], (C, C), jnp.float32, -s, s)
        W_k = jax.random.uniform(ks[2], (C, C), jnp.float32, -s, s)
        W_v = jax.random.uniform(ks[3], (C, C), jnp.float32, -s, s)
        mu_r = jax.random.uniform(ks[4], (C,), jnp.float32)
        mu_k = jax.random.uniform(ks[5], (C,), jnp.float32)
        return {'x': x, 'W_r': W_r, 'W_k': W_k, 'W_v': W_v, 'mu_r': mu_r, 'mu_k': mu_k}
    _L1_ffn_in = _L1_ffn_setup()

    def _L2_attn_setup():
        import jax, jax.numpy as jnp
        import numpy as np
        SCALING = 1.0
        H, N = (128, 64)
        B, L = (4, 256)
        key = jax.random.key(seed)
        ks = jax.random.split(key, 10)
        x = jax.random.normal(ks[0], (B, L, H), dtype=jnp.float32)
        in_proj = jax.random.normal(ks[1], (H, N), dtype=jnp.float32)
        out_proj = jax.random.normal(ks[2], (N, H), dtype=jnp.float32)
        lo, hi = (np.log(0.01), np.log(100.0))
        frequencies = jnp.exp(jax.random.uniform(ks[3], (N,)) * (hi - lo) + lo) / SCALING
        decays = jnp.full((N,), np.log(0.5), dtype=jnp.float32)
        s = 1.0 / np.sqrt(H)
        ss_W = jax.random.uniform(ks[4], (H, H), minval=-s, maxval=s)
        ss_b = jax.random.uniform(ks[5], (H,), minval=-s, maxval=s)
        gate_W = jax.random.uniform(ks[6], (H, H), minval=-s, maxval=s)
        gate_b = jax.random.uniform(ks[7], (H,), minval=-s, maxval=s)
        fin_W = jax.random.uniform(ks[8], (H, H), minval=-s, maxval=s)
        fin_b = jax.random.uniform(ks[9], (H,), minval=-s, maxval=s)
        return {'x': x, 'in_proj': in_proj, 'out_proj': out_proj, 'frequencies': frequencies, 'decays': decays, 'ss_W': ss_W, 'ss_b': ss_b, 'gate_W': gate_W, 'gate_b': gate_b, 'fin_W': fin_W, 'fin_b': fin_b}
    _L2_attn_in = _L2_attn_setup()

    def _L2_ffn_setup():
        import jax, jax.numpy as jnp
        import numpy as np
        H, E, DFF = (128, 8, 512)
        key = jax.random.key(seed)
        ks = jax.random.split(key, 7)
        s = lambda *shape: 1.0 / np.sqrt(shape[-2] if len(shape) > 1 else shape[-1])
        x = jax.random.normal(ks[0], (2, 256, H), dtype=jnp.float32)
        Wr = jax.random.normal(ks[1], (H, E), dtype=jnp.float32) * (1.0 / np.sqrt(H))
        br = jnp.zeros((E,), dtype=jnp.float32)
        W1 = jax.random.normal(ks[2], (E, H, DFF), dtype=jnp.float32) * (1.0 / np.sqrt(H))
        b1 = jnp.zeros((E, DFF), dtype=jnp.float32)
        W2 = jax.random.normal(ks[3], (E, DFF, H), dtype=jnp.float32) * (1.0 / np.sqrt(DFF))
        b2 = jnp.zeros((E, H), dtype=jnp.float32)
        return {'x': x, 'Wr': Wr, 'br': br, 'W1': W1, 'b1': b1, 'W2': W2, 'b2': b2}
    _L2_ffn_in = _L2_ffn_setup()

    def _L3_attn_setup():
        import jax, jax.numpy as jnp
        import numpy as np
        key = jax.random.key(seed)
        k_u, k_wl, k_b, k_c = jax.random.split(key, 4)
        B_, T, D, N = (4, 512, 128, 32)
        u = jax.random.normal(k_u, (B_, T, D), dtype=jnp.float32)
        Wl = jax.random.normal(k_wl, (N, D), dtype=jnp.float32) * 0.02
        bl = jnp.full((N,), 2.0, dtype=jnp.float32)
        xav_b = 0.5 * np.sqrt(6.0 / (D + N))
        Wb = jax.random.uniform(k_b, (N, D), dtype=jnp.float32, minval=-xav_b, maxval=xav_b)
        xav_c = 0.5 * np.sqrt(6.0 / (N + D))
        Wc = jax.random.uniform(k_c, (D, N), dtype=jnp.float32, minval=-xav_c, maxval=xav_c)
        Dp = jnp.zeros((D,), dtype=jnp.float32)
        return {'u': u, 'Wl': Wl, 'bl': bl, 'Wb': Wb, 'Wc': Wc, 'Dp': Dp}
    _L3_attn_in = _L3_attn_setup()

    def _L3_ffn_setup():
        import jax, jax.numpy as jnp
        import numpy as np
        D = 128
        H = 16
        HD = D // H
        L = 64
        E = 8
        B, T = (4, 256)
        EPS = 1e-06

        def _glorot(k, shape):
            fan_in, fan_out = (shape[-2], shape[-1])
            lim = np.sqrt(6.0 / (fan_in + fan_out)).astype(np.float32)
            return jax.random.uniform(k, shape, jnp.float32, -lim, lim)

        def _rmsnorm(x, gamma):
            return gamma * x * jax.lax.rsqrt(jnp.mean(x * x, axis=-1, keepdims=True) + EPS)
        key = jax.random.key(seed)
        ks = jax.random.split(key, 8)
        return {'x': jax.random.normal(ks[0], (B, T, D), jnp.float32), 'gamma1': jnp.ones((D,), jnp.float32), 'Wq': _glorot(ks[1], (D, D)), 'bq': jnp.zeros((D,), jnp.float32), 'Wdown': _glorot(ks[2], (D, L)), 'bdown': jnp.zeros((L,), jnp.float32), 'Wup': _glorot(ks[3], (L, 2 * D)), 'bup': jnp.zeros((2 * D,), jnp.float32), 'Wo': _glorot(ks[4], (D, D)), 'bo': jnp.zeros((D,), jnp.float32), 'gamma2': jnp.ones((D,), jnp.float32), 'Wg': _glorot(ks[5], (D, E)), 'bg': jnp.zeros((E,), jnp.float32), 'We': _glorot(ks[6], (E, D, D))}
    _L3_ffn_in = _L3_ffn_setup()
    _d = {'L0_attn_x': _L0_attn_in['x'], 'L0_attn_w0': _L0_attn_in['w0'], 'L0_attn_w1': _L0_attn_in['w1'], 'L0_attn_w2': _L0_attn_in['w2'], 'L0_ffn_expert_sel': _L0_ffn_in['expert_sel'], 'L0_ffn_keys': _L0_ffn_in['keys'], 'L0_ffn_values': _L0_ffn_in['values'], 'L1_attn_Wqkv': _L1_attn_in['Wqkv'], 'L1_attn_bqkv': _L1_attn_in['bqkv'], 'L1_attn_gq': _L1_attn_in['gq'], 'L1_attn_gk': _L1_attn_in['gk'], 'L1_attn_Wout': _L1_attn_in['Wout'], 'L1_attn_bout': _L1_attn_in['bout'], 'L1_attn_gout': _L1_attn_in['gout'], 'L1_ffn_W_r': _L1_ffn_in['W_r'], 'L1_ffn_W_k': _L1_ffn_in['W_k'], 'L1_ffn_W_v': _L1_ffn_in['W_v'], 'L1_ffn_mu_r': _L1_ffn_in['mu_r'], 'L1_ffn_mu_k': _L1_ffn_in['mu_k'], 'L2_attn_in_proj': _L2_attn_in['in_proj'], 'L2_attn_out_proj': _L2_attn_in['out_proj'], 'L2_attn_frequencies': _L2_attn_in['frequencies'], 'L2_attn_decays': _L2_attn_in['decays'], 'L2_attn_ss_W': _L2_attn_in['ss_W'], 'L2_attn_ss_b': _L2_attn_in['ss_b'], 'L2_attn_gate_W': _L2_attn_in['gate_W'], 'L2_attn_gate_b': _L2_attn_in['gate_b'], 'L2_attn_fin_W': _L2_attn_in['fin_W'], 'L2_attn_fin_b': _L2_attn_in['fin_b'], 'L2_ffn_Wr': _L2_ffn_in['Wr'], 'L2_ffn_br': _L2_ffn_in['br'], 'L2_ffn_W1': _L2_ffn_in['W1'], 'L2_ffn_b1': _L2_ffn_in['b1'], 'L2_ffn_W2': _L2_ffn_in['W2'], 'L2_ffn_b2': _L2_ffn_in['b2'], 'L3_attn_Wl': _L3_attn_in['Wl'], 'L3_attn_bl': _L3_attn_in['bl'], 'L3_attn_Wb': _L3_attn_in['Wb'], 'L3_attn_Wc': _L3_attn_in['Wc'], 'L3_attn_Dp': _L3_attn_in['Dp'], 'L3_ffn_gamma1': _L3_ffn_in['gamma1'], 'L3_ffn_Wq': _L3_ffn_in['Wq'], 'L3_ffn_bq': _L3_ffn_in['bq'], 'L3_ffn_Wdown': _L3_ffn_in['Wdown'], 'L3_ffn_bdown': _L3_ffn_in['bdown'], 'L3_ffn_Wup': _L3_ffn_in['Wup'], 'L3_ffn_bup': _L3_ffn_in['bup'], 'L3_ffn_Wo': _L3_ffn_in['Wo'], 'L3_ffn_bo': _L3_ffn_in['bo'], 'L3_ffn_gamma2': _L3_ffn_in['gamma2'], 'L3_ffn_Wg': _L3_ffn_in['Wg'], 'L3_ffn_bg': _L3_ffn_in['bg'], 'L3_ffn_We': _L3_ffn_in['We']}
    _x0 = _d['L0_attn_x']
    _d['L0_attn_x'] = jax.random.normal(jax.random.fold_in(jax.random.key(seed), 1), (8, 512, 128), dtype=_x0.dtype)
    del _x0
    return _d

def reference(L0_attn_x, L0_attn_w0, L0_attn_w1, L0_attn_w2, L0_ffn_expert_sel, L0_ffn_keys, L0_ffn_values, L1_attn_Wqkv, L1_attn_bqkv, L1_attn_gq, L1_attn_gk, L1_attn_Wout, L1_attn_bout, L1_attn_gout, L1_ffn_W_r, L1_ffn_W_k, L1_ffn_W_v, L1_ffn_mu_r, L1_ffn_mu_k, L2_attn_in_proj, L2_attn_out_proj, L2_attn_frequencies, L2_attn_decays, L2_attn_ss_W, L2_attn_ss_b, L2_attn_gate_W, L2_attn_gate_b, L2_attn_fin_W, L2_attn_fin_b, L2_ffn_Wr, L2_ffn_br, L2_ffn_W1, L2_ffn_b1, L2_ffn_W2, L2_ffn_b2, L3_attn_Wl, L3_attn_bl, L3_attn_Wb, L3_attn_Wc, L3_attn_Dp, L3_ffn_gamma1, L3_ffn_Wq, L3_ffn_bq, L3_ffn_Wdown, L3_ffn_bdown, L3_ffn_Wup, L3_ffn_bup, L3_ffn_Wo, L3_ffn_bo, L3_ffn_gamma2, L3_ffn_Wg, L3_ffn_bg, L3_ffn_We):

    def _L0_attn_ref(x, w0, w1, w2):
        import jax, jax.numpy as jnp
        import numpy as np
        CHUNK = 64
        LR = 0.001

        def _fast_weight(xc, a0, a1, a2):
            h = jax.nn.silu(jnp.einsum('bch,hf->bcf', xc, a0)) * jnp.einsum('bch,hf->bcf', xc, a2)
            return jnp.einsum('bcf,fh->bch', h, a1)

        def _reference_tuple_inner(x, w0, w1, w2):
            B, S, H = x.shape
            nC = S // CHUNK
            xc = x.reshape(B, nC, CHUNK, H).transpose(1, 0, 2, 3)

            def step(carry, x_chunk):
                a0, a1, a2, acc_loss = carry
                out = _fast_weight(x_chunk, a0, a1, a2)
                chunk_loss = jnp.mean((out - x_chunk) ** 2)
                decay = 1.0 - LR * chunk_loss
                return ((a0 * decay, a1 * decay, a2 * decay, acc_loss + chunk_loss), out)
            init = (w0, w1, w2, jnp.float32(0.0))
            (_, _, _, total_loss), outs = jax.lax.scan(step, init, xc)
            output = outs.transpose(1, 0, 2, 3).reshape(B, S, H)
            return (output, total_loss / nC)
        return _reference_tuple_inner(x, w0, w1, w2)[0]

    def _L0_ffn_ref(x, expert_sel, keys, values):
        import jax, jax.numpy as jnp
        import numpy as np
        N_HEADS = 4
        B, S, d = x.shape
        n_experts = keys.shape[0]
        xf = x.reshape(-1, d)
        N = xf.shape[0]
        logits = xf @ expert_sel.T
        sel = jax.nn.sigmoid(logits)
        sel_val, sel_idx = jax.lax.top_k(sel, N_HEADS)
        gates = jnp.zeros((N, n_experts), dtype=x.dtype)
        gates = gates.at[jnp.arange(N)[:, None], sel_idx].set(sel_val)
        h = jnp.einsum('nd,kde->nke', xf, keys)
        scores = jax.nn.relu(h) * gates[:, :, None]
        out = jnp.einsum('nke,kev->nv', scores, values)
        return out.reshape(B, S, -1)

    def _L1_attn_ref(x, Wqkv, bqkv, gq, gk, Wout, bout, gout):
        import jax, jax.numpy as jnp
        import numpy as np
        DIM = 128
        NUM_HEAD = 16
        DIM_HEAD = DIM // NUM_HEAD
        RMS_EPS = 1.1920929e-07
        EPS_LIN = 1e-06
        THETA = 10000.0

        def rmsnorm(x, g, eps=RMS_EPS):
            return x * jax.lax.rsqrt(jnp.mean(x * x, axis=-1, keepdims=True) + eps) * g

        def rope_cos_sin(seq_len, dim_head, dtype=jnp.float32):
            inv_freq = 1.0 / THETA ** (jnp.arange(0, dim_head, 2, dtype=dtype) / dim_head)
            t = jnp.arange(seq_len, dtype=dtype)
            freqs = jnp.outer(t, inv_freq)
            return (jnp.cos(freqs), jnp.sin(freqs))

        def apply_rope(t, cos, sin):
            tr = t[..., 0::2]
            ti = t[..., 1::2]
            out_r = tr * cos - ti * sin
            out_i = tr * sin + ti * cos
            return jnp.stack([out_r, out_i], axis=-1).reshape(t.shape)
        B, L, D = x.shape
        qkv = x @ Wqkv.T + bqkv
        q, k, v = jnp.split(qkv, 3, axis=-1)
        q = rmsnorm(q, gq)
        k = rmsnorm(k, gk)
        split = lambda t: t.reshape(B, L, NUM_HEAD, DIM_HEAD).transpose(0, 2, 1, 3)
        q, k, v = (split(q), split(k), split(v))
        cos, sin = rope_cos_sin(L, DIM_HEAD)
        cos = cos[None, None]
        sin = sin[None, None]
        q = apply_rope(q, cos, sin)
        k = apply_rope(k, cos, sin)
        qf = jax.nn.relu(q)
        kf = jax.nn.relu(k)
        vpad = jnp.concatenate([v, jnp.ones_like(v[..., :1])], axis=-1)
        vk = jnp.einsum('bhlp,bhld->bhpd', vpad, kf)
        res = jnp.einsum('bhpd,bhld->bhlp', vk, qf)
        attn = res[..., :-1] / (res[..., -1:] + EPS_LIN)
        attn = attn.transpose(0, 2, 1, 3).reshape(B, L, D)
        out = rmsnorm(attn @ Wout.T + bout, gout)
        return out

    def _L1_ffn_ref(x, W_r, W_k, W_v, mu_r, mu_k):
        import jax, jax.numpy as jnp
        import numpy as np
        DIM = 128

        def _reference_tuple_inner(x, W_r, W_k, W_v, mu_r, mu_k):
            B, T, C = x.shape
            x_prev = jnp.concatenate([jnp.zeros((B, 1, C), x.dtype), x[:, :-1, :]], axis=1)
            xr = mu_r * x + (1.0 - mu_r) * x_prev
            xk = mu_k * x + (1.0 - mu_k) * x_prev
            r = jax.nn.sigmoid(jnp.einsum('btc,dc->btd', xr, W_r))
            k = jnp.einsum('btc,dc->btd', xk, W_k)
            k_act = jnp.square(jax.nn.relu(k))
            out = r * jnp.einsum('btc,dc->btd', k_act, W_v)
            new_state = x[:, -1, :]
            return (out, new_state)
        return _reference_tuple_inner(x, W_r, W_k, W_v, mu_r, mu_k)[0]

    def _L2_attn_ref(x, in_proj, out_proj, frequencies, decays, ss_W, ss_b, gate_W, gate_b, fin_W, fin_b):
        import jax, jax.numpy as jnp
        import numpy as np
        SCALING = 1.0
        B, L, H = x.shape
        fft_len = 2 * L - 1
        freqs = frequencies * (2.0 * jnp.pi * SCALING)
        dec = -jnp.exp(decays) * SCALING
        lam = dec + 1j * freqs
        kernel = jnp.exp(lam[None, :] * jnp.arange(L, dtype=jnp.float32)[:, None])
        k = jnp.einsum('hn,kn,nh->hk', in_proj.astype(kernel.dtype), kernel, out_proj.astype(kernel.dtype)).real
        u = jnp.transpose(x, (0, 2, 1))
        u_f = jnp.fft.fft(u, n=fft_len, axis=-1)
        k_f = jnp.fft.fft(k, n=fft_len, axis=-1)
        conv = jnp.fft.ifft(u_f * k_f[None], axis=-1)[:, :, :L].real
        ss_out = jnp.transpose(conv, (0, 2, 1))
        ss_out = jax.nn.gelu(ss_out @ ss_W.T + ss_b, approximate=False)
        gate = jax.nn.gelu(x @ gate_W.T + gate_b, approximate=False)
        return gate * ss_out @ fin_W.T + fin_b

    def _L2_ffn_ref(x, Wr, br, W1, b1, W2, b2):
        import jax, jax.numpy as jnp
        import numpy as np
        H, E, DFF = (128, 8, 512)
        B, S, Hd = x.shape
        n_exp = W1.shape[0]
        xt = x.reshape(-1, Hd)
        logits = xt @ Wr + br
        probs = jax.nn.softmax(logits, axis=-1)
        gate = jnp.max(probs, axis=-1)
        idx = jnp.argmax(probs, axis=-1)
        h1 = jnp.maximum(jnp.einsum('th,ehf->etf', xt, W1) + b1[:, None, :], 0.0)
        ye = jnp.einsum('etf,efh->eth', h1, W2) + b2[:, None, :]
        onehot = jax.nn.one_hot(idx, n_exp, dtype=xt.dtype)
        y = jnp.einsum('te,eth->th', onehot, ye) * gate[:, None]
        return y.reshape(B, S, Hd)

    def _L3_attn_ref(u, Wl, bl, Wb, Wc, Dp):
        import jax, jax.numpy as jnp
        import numpy as np
        lam = jax.nn.sigmoid(jnp.einsum('btd,nd->btn', u, Wl) + bl)
        Bu = jnp.einsum('btd,nd->btn', u, Wb)

        def step(h, inp):
            lam_t, bu_t = inp
            h = lam_t * h + bu_t
            return (h, h)
        h0 = jnp.zeros((u.shape[0], Wl.shape[0]), dtype=u.dtype)
        _, H = jax.lax.scan(step, h0, (jnp.swapaxes(lam, 0, 1), jnp.swapaxes(Bu, 0, 1)))
        H = jnp.swapaxes(H, 0, 1)
        y = jnp.einsum('btn,dn->btd', H, Wc) + u * Dp
        return y

    def _L3_ffn_ref(x, gamma1, Wq, bq, Wdown, bdown, Wup, bup, Wo, bo, gamma2, Wg, bg, We):
        import jax, jax.numpy as jnp
        import numpy as np
        D = 128
        H = 16
        HD = D // H
        L = 64
        E = 8
        B, T = (4, 256)
        EPS = 1e-06

        def _glorot(k, shape):
            fan_in, fan_out = (shape[-2], shape[-1])
            lim = np.sqrt(6.0 / (fan_in + fan_out)).astype(np.float32)
            return jax.random.uniform(k, shape, jnp.float32, -lim, lim)

        def _rmsnorm(x, gamma):
            return gamma * x * jax.lax.rsqrt(jnp.mean(x * x, axis=-1, keepdims=True) + EPS)
        b, t = (x.shape[0], x.shape[1])
        h = _rmsnorm(x, gamma1)
        q = (h @ Wq + bq).reshape(b, t, H, HD)
        kv = ((h @ Wdown + bdown) @ Wup + bup).reshape(b, t, H, 2 * HD)
        k, v = jnp.split(kv, 2, axis=-1)
        att = jnp.einsum('bthd,btgd->bthg', q, k) / np.sqrt(HD).astype(np.float32)
        att = jax.nn.softmax(att, axis=-1)
        out = jnp.einsum('bthg,btgd->bthd', att, v).reshape(b, t, D)
        x = x + (out @ Wo + bo)
        h2 = _rmsnorm(x, gamma2)
        gate = jax.nn.softmax(h2 @ Wg + bg, axis=-1)
        combined = jnp.einsum('btd,edf,bte->btf', h2, We, gate)
        return x + combined
    x = L0_attn_x
    xn = _layernorm(x, axis=-1)
    x = x + _L0_attn_ref(xn, L0_attn_w0, L0_attn_w1, L0_attn_w2) + _L0_ffn_ref(xn, L0_ffn_expert_sel, L0_ffn_keys, L0_ffn_values)
    xn = _layernorm(x, axis=-1)
    x = x + _L1_attn_ref(xn, L1_attn_Wqkv, L1_attn_bqkv, L1_attn_gq, L1_attn_gk, L1_attn_Wout, L1_attn_bout, L1_attn_gout) + _L1_ffn_ref(xn, L1_ffn_W_r, L1_ffn_W_k, L1_ffn_W_v, L1_ffn_mu_r, L1_ffn_mu_k)
    xn = _layernorm(x, axis=-1)
    x = x + _L2_attn_ref(xn, L2_attn_in_proj, L2_attn_out_proj, L2_attn_frequencies, L2_attn_decays, L2_attn_ss_W, L2_attn_ss_b, L2_attn_gate_W, L2_attn_gate_b, L2_attn_fin_W, L2_attn_fin_b) + _L2_ffn_ref(xn, L2_ffn_Wr, L2_ffn_br, L2_ffn_W1, L2_ffn_b1, L2_ffn_W2, L2_ffn_b2)
    xn = _layernorm(x, axis=-1)
    x = x + _L3_attn_ref(xn, L3_attn_Wl, L3_attn_bl, L3_attn_Wb, L3_attn_Wc, L3_attn_Dp) + _L3_ffn_ref(xn, L3_ffn_gamma1, L3_ffn_Wq, L3_ffn_bq, L3_ffn_Wdown, L3_ffn_bdown, L3_ffn_Wup, L3_ffn_bup, L3_ffn_Wo, L3_ffn_bo, L3_ffn_gamma2, L3_ffn_Wg, L3_ffn_bg, L3_ffn_We)
    return x

_drawn_inputs = setup_inputs


def setup_inputs(seed=0):
    import zlib

    import numpy as np

    out = dict(_drawn_inputs(seed))
    spreads = {'L1_attn_gq': (1.0, 0.6),
     'L1_attn_gk': (1.0, 0.577),
     'L1_attn_gout': (1.0, 0.2),
     'L2_attn_decays': (-0.6931471824645996, 0.568),
     'L2_ffn_br': (0.0, 0.1),
     'L2_ffn_b1': (0.0, 0.484),
     'L2_ffn_b2': (0.0, 0.297),
     'L3_attn_bl': (2.0, 0.2),
     'L3_attn_Dp': (0.0, 0.277),
     'L3_ffn_gamma1': (1.0, 0.2),
     'L3_ffn_bq': (0.0, 0.8),
     'L3_ffn_bdown': (0.0, 0.678),
     'L3_ffn_bup': (0.0, 0.436),
     'L3_ffn_bo': (0.0, 0.1),
     'L3_ffn_gamma2': (1.0, 0.2),
     'L3_ffn_bg': (0.0, 0.394)}
    factors = {'L0_attn_w0': 3.597,
     'L0_attn_w1': 4.181,
     'L0_attn_w2': 3.994,
     'L1_ffn_W_r': 3.165,
     'L1_ffn_mu_r': 5.513,
     'L2_attn_ss_b': 8.0}
    for name, (base, spread) in spreads.items():
        noise = np.random.default_rng([zlib.crc32(name.encode()), seed]).standard_normal(out[name].shape)
        drawn = base * np.exp(spread * noise) if base else spread * noise
        out[name] = jnp.asarray(drawn.astype(out[name].dtype))
    for name, factor in factors.items():
        out[name] = (out[name] * factor).astype(out[name].dtype)
    return out
```

```python
from contextlib import ExitStack

import numpy as np

import concourse.bass as bass
from concourse import mybir

FP32 = mybir.dt.float32
BF16 = mybir.dt.bfloat16
I32 = mybir.dt.int32
U32 = mybir.dt.uint32
ALU = mybir.AluOpType
ACT = mybir.ActivationFunctionType
AX = mybir.AxisListType

B, T, D = 8, 512, 128
P = 128
N = B * T
TILES = N // P
TPB = T // P
LN_EPS, RMS_EPS1, EPS_LIN, RMS_EPS3 = 1e-5, 1.1920929e-07, 1e-6, 1e-6
F0, CHUNK, LR = 512, 64, 0.001
NCH = T // CHUNK
FC = F0 // P
E0, K0 = 64, 4
S0 = -(-(N * K0 // P + E0 - 1) // 8) * 8
E2, F2 = 8, 512
S2 = -(-(N // P + E2 - 1) // 4) * 4
NS = 64
NL = 32
H, HD = 16, 8
E3 = 8
LAT = 64

def constants():
    p = np.arange(P)
    parts = {}
    parts["ident"] = np.eye(P)
    parts["before"] = (p[:, None] < p[None, :]) * 1.0
    parts["headblock"] = (p[:, None] // HD == p[None, :] // HD) * 1.0
    parts["iota_e"] = np.tile(np.arange(64.0), (P, 1))
    parts["slot_id"] = np.stack([p, p + P], 1) * 1.0
    parts["head_in_group"] = (p[:, None] // HD % 4 == np.arange(4)[None, :]) * 1.0
    sel = np.zeros((P, 4, P))
    for g in range(4):
        for j in range(4):
            sel[32 * g + j, j, :] = 1.0
    parts["shift_sel"] = sel.reshape(P, 4 * P)
    inv = (1.0 / np.float32(10000.0) ** (np.arange(0, HD, 2, dtype=np.float32) / HD)).astype(np.float32)
    ang = np.outer(np.arange(T, dtype=np.float32), inv).astype(np.float32)
    c, s = np.cos(ang), np.sin(ang)
    c2 = np.stack([c, c], -1).reshape(TPB, P, HD)
    s2 = np.stack([-s, s], -1).reshape(TPB, P, HD)
    parts["rope_cos"] = c2.transpose(1, 0, 2).reshape(P, TPB * HD)
    parts["rope_sin"] = s2.transpose(1, 0, 2).reshape(P, TPB * HD)
    parts["lags"] = np.tile(np.concatenate([P - np.arange(P + 1.0), [P, P]]), (P, 1))
    parts["quarter"] = np.concatenate([np.tile((p < 64)[:, None] * 1.0, (1, P + 1)), np.ones((P, 1)), np.zeros((P, 1))], 1)
    parts["imag_sign"] = np.where(p < 64, 1.0, -1.0)[:, None]
    swap = np.zeros((P, P))
    swap[p, (p + 64) % P] = 1.0
    parts["swap_halves"] = swap
    at, cols, off = {}, [], 0
    for k, v in parts.items():
        at[k] = (off, v.shape[1])
        off += v.shape[1]
        cols.append(v.astype(np.float32))
    return np.ascontiguousarray(np.concatenate(cols, 1)), at


def program(nc, A, cst_dram, at, out, upto=99, dbg=None):
    ctx = ExitStack()
    with ctx:
        lasting = {n: ctx.enter_context(nc.semaphore(n)) for n in
                   ("stage_done", "stage_go", "plain_in", "slots_cleared", "experts0_in", "experts2_in",
                    "toeplitz0", "toeplitz1",
                    "sorted0", "sorted2", *(f"got{L}_{i}" for L in (0, 2) for i in range(4)))}
        of_stage = [ctx.enter_context(nc.semaphore(f"of_stage_{i}")) for i in range(64)]
        names_of_stage, current = {}, [0]

        def sem(name):
            if name in lasting:
                return lasting[name]
            names = names_of_stage.setdefault(current[0], [])
            if name not in names:
                names.append(name)
            return of_stage[names.index(name)]

        def sb(name, shape, dt=FP32):
            return ctx.enter_context(nc.sbuf_tensor(name, shape, dt))

        xT = sb("xT", [P, N])
        xn = sb("xn", [P, N])
        xtok = sb("xtok", [P, TILES, D])
        arena = sb("arena", [P, 16384])
        cst = sb("cst", [P, cst_dram.shape[1]])
        psum = ctx.enter_context(nc.psum_tensor("psum", [P, 8, 512], FP32))
        PS = [psum[:, i, :] for i in range(8)]
        pair_of_banks = [psum[:, 2 * i:2 * i + 2, :] for i in range(4)]

        def const(name):
            a, n = at[name]
            return cst[:, a:a + n]

        ident = const("ident")
        ones_mean = sb("ones_mean", [P, P])
        ones_loss = sb("ones_loss", [P, P])
        ones_bf = sb("ones_bf", [P, P], BF16)
        before_bf = sb("before_bf", [P, P], BF16)
        ident_bf = sb("ident_bf", [P, P], BF16)
        eps_ln = sb("eps_ln", [P, 1])
        eps_r1 = sb("eps_r1", [P, 1])
        eps_r3 = sb("eps_r3", [P, 1])

        pe_prog, act_prog, dve_prog, pool_prog, sp_prog = [], [], [], [], []
        stages = []

        def stage(pe=None, act=None, dve=None, pool=None, sp=None):
            stages.append((pe, act, dve, pool, sp))

        W0 = sb("W0", [P, F0])
        W1 = sb("W1", [P, FC, D])
        W2 = sb("W2", [P, F0])
        Wr2 = sb("Wr2", [P, E2])
        Wdown, Wup = sb("Wdown", [P, LAT]), sb("Wup", [LAT, 2 * D])
        Wq, Wo, Wg, We = sb("Wq", [P, D]), sb("Wo", [P, D]), sb("Wg", [P, E3]), sb("We", [P, E3, D])
        out_proj = sb("out_proj", [NS, D])
        b2 = sb("b2", [1, E2 * D])
        plain = [
            (W0[:], A["L0_attn_w0"]), (W1[:], A["L0_attn_w1"].rearrange("(c p) d -> p c d", p=P)),
            (W2[:], A["L0_attn_w2"]), (Wr2[:], A["L2_ffn_Wr"]), (Wdown[:], A["L3_ffn_Wdown"]),
            (Wup[:], A["L3_ffn_Wup"]), (Wq[:], A["L3_ffn_Wq"]), (Wo[:], A["L3_ffn_Wo"]),
            (Wg[:], A["L3_ffn_Wg"]), (We[:], A["L3_ffn_We"].rearrange("e i o -> i e o")),
            (out_proj[:], A["L2_attn_out_proj"]),
            (b2[:], A["L2_ffn_b2"].rearrange("(a e) d -> a (e d)", a=1)),
        ]
        vec_names = ["L1_attn_bout", "L1_attn_gout", "L1_ffn_mu_r", "L1_ffn_mu_k", "L2_attn_ss_b", "L2_attn_gate_b",
                     "L2_attn_fin_b", "L3_attn_Dp", "L3_ffn_gamma1", "L3_ffn_bq", "L3_ffn_bo", "L3_ffn_gamma2"]
        vecs = sb("vecs", [P, len(vec_names)])
        vec = {n: vecs[:, i:i + 1] for i, n in enumerate(vec_names)}
        for n in vec_names:
            plain.append((vec[n], A[n].rearrange("(p a) -> p a", a=1)))
        bdown = sb("bdown", [LAT, 1])
        plain.append((bdown[:], A["L3_ffn_bdown"].rearrange("(p a) -> p a", a=1)))
        bl4 = sb("bl4", [P, 1])
        freq, decay = sb("freq", [P, 1]), sb("decay", [P, 1])
        for g in range(4):
            plain.append((bl4[32 * g:32 * g + 32, :], A["L3_attn_bl"].rearrange("(p a) -> p a", a=1)))
        for g in range(2):
            plain.append((freq[64 * g:64 * g + 64, :], A["L2_attn_frequencies"].rearrange("(p a) -> p a", a=1)))
            plain.append((decay[64 * g:64 * g + 64, :], A["L2_attn_decays"].rearrange("(p a) -> p a", a=1)))
        row_names = [("L1_attn_bqkv", 384), ("L1_attn_gq", D), ("L1_attn_gk", D), ("L2_ffn_br", E2),
                     ("L3_ffn_bg", E3), ("L3_ffn_bq", D), ("L3_ffn_bup", 2 * D)]
        rows = {}
        for n, w in row_names:
            rows[n] = sb("row_" + n, [P, w])
            plain.append((rows[n][:], A[n].partition_broadcast(P)))
        turned = []
        for i in range(3):
            turned.append((f"qkv{i}", A["L1_attn_Wqkv"][i * D:(i + 1) * D, :], D, D))
        turned += [("sel", A["L0_ffn_expert_sel"], E0, D), ("out1", A["L1_attn_Wout"], D, D),
                   ("r", A["L1_ffn_W_r"], D, D), ("k", A["L1_ffn_W_k"], D, D), ("v", A["L1_ffn_W_v"], D, D),
                   ("ss", A["L2_attn_ss_W"], D, D), ("gate", A["L2_attn_gate_W"], D, D),
                   ("fin", A["L2_attn_fin_W"], D, D), ("in_proj", A["L2_attn_in_proj"], D, NS),
                   ("lam", A["L3_attn_Wl"], NL, D), ("bu", A["L3_attn_Wb"], NL, D),
                   ("c", A["L3_attn_Wc"], D, P),
                   ("b1", A["L2_ffn_b1"].rearrange("e (c p) -> (e c) p", p=P), E2 * F2 // P, P)]
        turnedT = sb("turnedT", [P, len(turned) * P])
        WT = {n: turnedT[0:c, i * P:i * P + r] for i, (n, _, r, c) in enumerate(turned)}
        natural = xn
        n_plain = len(plain) + 1
        keys = arena[:, 0:E0 * D].rearrange("p (e h) -> p e h", e=E0)
        values = arena[:, E0 * D:2 * E0 * D].rearrange("p (e h) -> p e h", e=E0)
        Xs0 = nc.dram_tensor("Xs0", (S0 * P, D), FP32).ap()
        Ys0 = nc.dram_tensor("Ys0", (S0 * P, D), FP32).ap()
        Xs2 = nc.dram_tensor("Xs2", (S2 * P, D), FP32).ap()
        Ys2 = nc.dram_tensor("Ys2", (S2 * P, D), FP32).ap()
        work = sb("work", [P, 8192])
        zero = work[:, 4096:4096 + 8 * D].rearrange("p (t d) -> p t d", d=D)
        TG = 4
        n_turn_groups = -(-len(turned) // TG)

        def setup_sp(sp):
            for b in range(B):
                sp.dma_start(xtok[:, b * TPB:(b + 1) * TPB, :],
                             A["L0_attn_x"][b].rearrange("(t p) d -> p t d", p=P)).then_inc(sem(f"x_in{b}"), 16)
            for d, s in plain:
                sp.dma_start(d, s).then_inc(sem("plain_in"), 16)

        def setup_act(act):
            act.dma_start(cst[:], cst_dram).then_inc(sem("cst_in"), 16)
            for i, (n, s, r, c) in enumerate(turned):
                for j in range(c // s.shape[1]):
                    w = s.shape[1]
                    act.dma_start(natural[0:r, i * P + j * w:i * P + (j + 1) * w], s).then_inc(sem("natural_in"), 16)
            for b in range(B):
                act.wait_ge(sem("x_turned"), b + 1)
                act.activation(xT[:, b * T:(b + 1) * T], PS[b % 2][:], ACT.Copy).then_inc(sem("xT_ready"), 1)

        def setup_pe(pe):
            pe.wait_ge(sem("cst_in"), 16)
            for b in range(B):
                pe.wait_ge(sem(f"x_in{b}"), 16)
                if b >= 2:
                    pe.wait_ge(sem("xT_ready"), b - 1)
                for t in range(TPB):
                    last = pe.transpose(PS[b % 2][:, t * P:(t + 1) * P], xtok[:, b * TPB + t, :], ident)
                last.then_inc(sem("x_turned"), 1)
            pe.wait_ge(sem("natural_in"), 16 * (len(turned) + 3))
            pe.wait_ge(sem("consts_made"), 1)
            for g in range(n_turn_groups):
                if g >= 2:
                    pe.wait_ge(sem("w_evacuated"), g - 1)
                for j, (n, s, r, c) in enumerate(turned[g * TG:(g + 1) * TG]):
                    i = g * TG + j
                    last = pe.transpose(PS[2 + g % 2][0:c, j * P:j * P + r], natural[0:r, i * P:i * P + c],
                                        ident[0:r, 0:r])
                last.then_inc(sem("w_turned"), 1)

        def setup_dve(dve):
            dve.memset(ones_mean[:], 1.0 / D)
            dve.memset(ones_loss[:], 1.0 / (B * CHUNK * D))
            dve.memset(ones_bf[:], 1.0)
            dve.memset(one_row[:], 1.0)
            dve.memset(eps_ln[:], LN_EPS)
            dve.memset(eps_r1[:], RMS_EPS1)
            dve.memset(eps_r3[:], RMS_EPS3)
            dve.memset(turnedT[:], 0.0).then_inc(sem("turned_cleared"), 1)
            dve.wait_ge(sem("cst_in"), 16)
            dve.tensor_copy(before_bf[:], const("before"))
            dve.tensor_copy(ident_bf[:], const("ident")).then_inc(sem("consts_made"), 1)
            dve.wait_ge(sem("turned_cleared"), 1)
            for g in range(n_turn_groups):
                dve.wait_ge(sem("w_turned"), g + 1)
                for j, (n, s, r, c) in enumerate(turned[g * TG:(g + 1) * TG]):
                    last = dve.tensor_copy(WT[n], PS[2 + g % 2][0:c, j * P:j * P + r])
                last.then_inc(sem("w_evacuated"), 1)

        def setup_pool(pool):
            pool.memset(zero, 0.0)
        n_cleared = 16 * (S0 // 8 + S2 // 4)
        stage(setup_pe, setup_act, setup_dve, setup_pool, setup_sp)

        centred = work[:, 0:3 * T].rearrange("p (r n) -> p r n", r=3)
        squared = work[:, 3 * T:5 * T].rearrange("p (r n) -> p r n", r=2)
        ln_inverse = work[:, 5 * T:5 * T + TILES]

        def cols(buf, b):
            return buf[:, b * T:(b + 1) * T]

        def clear_slots(sp):
            for i in range(S0 // 8):
                sp.dma_start(Xs0[i * 8 * P:(i + 1) * 8 * P, :].rearrange("(t p) d -> p t d", p=P),
                             zero).then_inc(sem("slots_cleared"), 16)
            for i in range(S2 // 4):
                sp.dma_start(Xs2[i * 4 * P:(i + 1) * 4 * P, :].rearrange("(t p) d -> p t d", p=P),
                             zero[:, 0:4, :]).then_inc(sem("slots_cleared"), 16)

        def layer_norm(L, token_major):
            s = lambda n: sem(f"ln_{n}")

            def pe_mean(pe, b):
                if b >= 2:
                    pe.wait_ge(s("centred"), b - 1)
                pe.matmul(PS[b % 2][:], ones_mean[:], cols(xT, b), start=True, stop=True).then_inc(s("mean"), 1)

            def pe_var(pe, b):
                pe.wait_ge(s("squared"), b + 1)
                if b >= 2:
                    pe.wait_ge(s("deviation"), b - 1)
                for t in range(TPB):
                    last = pe.matmul(PS[2 + b % 2][:, t:t + 1], squared[:, b % 2, t * P:(t + 1) * P], ones_mean[:, 0:1],
                                     start=True, stop=True)
                last.then_inc(s("var"), 1)

            def pe_spread(pe, b):
                pe.wait_ge(s("inverse"), b + 1)
                if b >= 2:
                    pe.wait_ge(s("xn"), b - 1)
                for t in range(TPB):
                    last = pe.matmul(PS[6 + b % 2][:, t * P:(t + 1) * P], ln_inverse[:, b * TPB + t:b * TPB + t + 1].broadcast_to([P, P]), ident,
                                     start=True, stop=True)
                last.then_inc(s("spread"), 1)

            def pe_turn(pe, b):
                pe.wait_ge(s("xn"), b + 1)
                if b >= 2:
                    pe.wait_ge(s("xtok"), b - 1)
                for t in range(TPB):
                    last = pe.transpose(PS[4 + b % 2][:, t * P:(t + 1) * P],
                                        xn[:, b * T + t * P:b * T + (t + 1) * P], ident)
                last.then_inc(s("turned"), 1)

            def act_square(act, b):
                act.wait_ge(s("centred"), b + 1)
                if b >= 2:
                    act.wait_ge(s("var"), b - 1)
                act.activation(squared[:, b % 2, :], centred[:, b % 3, :], ACT.Square).then_inc(s("squared"), 1)

            def act_deviation(act, b):
                act.wait_ge(s("var"), b + 1)
                act.activation(ln_inverse[:, b * TPB:(b + 1) * TPB], PS[2 + b % 2][:, 0:TPB], ACT.Sqrt, bias=eps_ln[:]).then_inc(s("deviation"), 1)

            def act_tok(act, b):
                act.wait_ge(s("turned"), b + 1)
                act.activation(xtok[:, b * TPB:(b + 1) * TPB, :],
                               PS[4 + b % 2][:].rearrange("p (t d) -> p t d", d=D), ACT.Copy).then_inc(s("xtok"), 1)

            def dve_centre(dve, b):
                dve.wait_ge(s("mean"), b + 1)
                if b >= 3:
                    dve.wait_ge(s("squared"), b - 2)
                    dve.wait_ge(s("xn"), b - 2)
                dve.tensor_tensor(centred[:, b % 3, :], cols(xT, b), PS[b % 2][:], ALU.subtract).then_inc(s("centred"), 1)

            def dve_invert(dve, b):
                mine = ln_inverse[:, b * TPB:(b + 1) * TPB]
                dve.wait_ge(s("deviation"), b + 1)
                dve.reciprocal(mine, mine).then_inc(s("inverse"), 1)

            def dve_scale(dve, b):
                dve.wait_ge(s("spread"), b + 1)
                dve.tensor_tensor(cols(xn, b), centred[:, b % 3, :], PS[6 + b % 2][:], ALU.mult).then_inc(s("xn"), 1)

            def in_turn(eng, steps):
                for i in range(B + 3):
                    for k, step in steps:
                        if 0 <= i - k < B:
                            step(eng, i - k)

            def pe_prog(pe):
                in_turn(pe, [(0, pe_mean), (1, pe_var), (2, pe_spread)] + ([(3, pe_turn)] if token_major else []))

            def act_prog(act):
                in_turn(act, [(0, act_square), (1, act_deviation)] + ([(3, act_tok)] if token_major else []))

            def dve_prog(dve):
                in_turn(dve, [(0, dve_centre), (1, dve_invert), (2, dve_scale)])

            def sp_prog(sp):
                if L == 0:
                    clear_slots(sp)
                if L == 2:
                    layer2_loads(sp)

            stage(pe_prog, act_prog, dve_prog, None, sp_prog)


        def routing(L, E, K, selT, logit_bias, slots, Xs, logits, top8, gates_act, row_scale, buf, gates_dve=None):
            s = lambda n: sem(f"route_{n}")
            W = TILES * E
            idx8 = ctx.enter_context(nc.sbuf_tensor(f"idx8_{L}", [P, TILES, 8], U32))
            idxf = sb(f"idxf{L}", [P, K, TILES])
            place = [sb(f"place{L}_{k}", [P, TILES], I32) for k in range(K)]
            placef = sb(f"placef{L}", [P, K, TILES])
            lt = work[0:E, 0:2 * T].rearrange("p (r n) -> p r n", r=2)
            hot = buf[:, 4 * W + 256:4 * W + 256 + (K + 1) * W // 2].bitcast(BF16).rearrange("p (k t e) -> p k t e", k=K + 1, e=E)
            flat_counts, flat_running, flat_restart = (buf[:, i * W:(i + 1) * W] for i in range(3))
            counts, running, restart = (x.rearrange("p (e t) -> p e t", e=E) for x in (flat_counts, flat_running, flat_restart))
            position = buf[:, 3 * W:4 * W].rearrange("p (t e) -> p t e", e=E)
            picked = flat_restart.rearrange("p (t e) -> p t e", e=E)
            small = sb(f"small{L}", [P, 6, 64])
            small_i = sb(f"small_i{L}", [P, 2, 64], I32)
            NC = 2
            cmp_ = buf[:, 4 * W:4 * W + NC * E].rearrange("p (c e) -> p c e", e=E)
            expert_of = sb(f"expert_of{L}", [P, NC])
            expert_row = sb(f"expert_row{L}", [1, NC * P], I32)
            gw = min(W, 512)
            groups = W // gw
            tg = gw // E

            def pe_prog(pe):
                for b in range(B):
                    if b >= 2:
                        pe.wait_ge(s("logitsT"), b - 1)
                    pe.matmul(PS[b % 2][0:E, :], selT, cols(xn, b), start=True, stop=True).then_inc(s("scores"), 1)
                    if b >= 1:
                        turn(pe, b - 1)
                turn(pe, B - 1)
                pe.wait_ge(s("chosen"), 1)
                for g in range(groups):
                    m = hot[:, K, g * tg:(g + 1) * tg, :].rearrange("p t e -> p (t e)")
                    if g >= 4:
                        pe.wait_ge(s("counted"), 2 * (g - 3))
                    pe.matmul(PS[g][:, 0:gw], before_bf[:], m, start=True, stop=True)
                    pe.matmul(PS[4 + g][:, 0:gw], ones_bf[:], m, start=True, stop=True).then_inc(s("counts"), 1)
                pe.wait_ge(s("expert_of"), 1)
                for c in range(NC):
                    last = pe.matmul(PS[0][0:1, c * P:(c + 1) * P], expert_of[:, c:c + 1], ident, start=True, stop=True)
                last.then_inc(s("expert_turned"), 1)

            def turn(pe, b):
                pe.wait_ge(s("logitsT"), b + 1)
                if b >= 2:
                    pe.wait_ge(s("logits"), b - 1)
                for t in range(TPB):
                    last = pe.transpose(PS[2 + b % 2][:, t * E:(t + 1) * E], lt[:, b % 2, t * P:(t + 1) * P], ident[0:E, 0:E])
                last.then_inc(s("turned"), 1)

            def act_prog(act):
                for b in range(B):
                    act.wait_ge(s("scores"), b + 1)
                    if b >= 2:
                        act.wait_ge(s("turned"), b - 1)
                    act.activation(lt[:, b % 2, :], PS[b % 2][0:E, :], ACT.Copy).then_inc(s("logitsT"), 1)
                gates_act(act, s)

            def dve_prog(dve):
                for b in range(B):
                    dve.wait_ge(s("turned"), b + 1)
                    src = PS[2 + b % 2][:, 0:TPB * E].rearrange("p (t e) -> p t e", e=E)
                    dst = logits[:, b * TPB:(b + 1) * TPB, :]
                    if logit_bias is None:
                        dve.tensor_copy(dst, src).then_inc(s("logits"), 1)
                    else:
                        dve.tensor_tensor(dst, src, logit_bias.unsqueeze(1).broadcast_to([P, TPB, E]), ALU.add).then_inc(s("logits"), 1)
                dve.wait_ge(s("logits"), B)
                for t in range(TILES):
                    dve.max(top8[:, t, :], logits[:, t, :]).then_inc(s("top8"), 1)
                for t in range(TILES):
                    dve.wait_ge(s("top8"), t + 1)
                    dve.max_index(idx8[:, t, :], top8[:, t, :], logits[:, t, :]).then_inc(s("idx8"), 1)
                dve.wait_ge(s("idx8"), TILES)
                dve.tensor_copy(idxf[:], idx8[:, :, 0:K].rearrange("p t k -> p k t")).then_inc(s("idxf"), 1)
                dve.wait_ge(s("idxf"), 1)
                iota = const("iota_e")[:, 0:E].unsqueeze(1).broadcast_to([P, TILES, E])
                for k in range(K):
                    dve.tensor_tensor(hot[:, k, :, :], iota, idxf[:, k, :].unsqueeze(2).broadcast_to([P, TILES, E]),
                                      ALU.is_equal).then_inc(s("hot"), 1)
                dve.wait_ge(s("hot"), K)
                if K == 1:
                    dve.tensor_copy(hot[:, K, :, :], hot[:, 0, :, :]).then_inc(s("chosen"), 1)
                else:
                    assert K == 4
                    dve.tensor_tensor(hot[:, K, :, :], hot[:, 0, :, :], hot[:, 1, :, :], ALU.add).then_inc(s("sum"), 1)
                    dve.wait_ge(s("sum"), 1)
                    dve.tensor_tensor(hot[:, K, :, :], hot[:, K, :, :], hot[:, 2, :, :], ALU.add).then_inc(s("sum"), 1)
                    dve.wait_ge(s("sum"), 2)
                    dve.tensor_tensor(hot[:, K, :, :], hot[:, K, :, :], hot[:, 3, :, :], ALU.add).then_inc(s("chosen"), 1)
                dve.memset(restart, 1.0).then_inc(s("restart"), 1)
                dve.wait_ge(s("restart"), 1)
                dve.memset(restart[:, :, 0:1], 0.0).then_inc(s("restart"), 1)
                for g in range(groups):
                    dve.wait_ge(s("counts"), g + 1)
                    dve.tensor_copy(counts[:, :, g * tg:(g + 1) * tg],
                                    PS[4 + g][:, 0:gw].rearrange("p (t e) -> p e t", e=E)).then_inc(s("counted"), 1)
                    dve.tensor_copy(position[:, g * tg:(g + 1) * tg, :],
                                    PS[g][:, 0:gw].rearrange("p (t e) -> p t e", e=E)).then_inc(s("counted"), 1)
                dve.wait_ge(s("counted"), 2 * groups)
                dve.wait_ge(s("restart"), 2)
                dve.tensor_tensor_scan(flat_running, flat_restart, flat_counts, 0.0,
                                       ALU.mult, ALU.add).then_inc(s("running"), 1)
                dve.wait_ge(s("running"), 1)
                sm = lambda i: small[:, i, 0:E]
                dve.tensor_scalar(small_i[:, 0, 0:E], running[:, :, TILES - 1], float(P - 1), None, ALU.add).then_inc(s("tiles"), 1)
                dve.wait_ge(s("tiles"), 1)
                dve.tensor_scalar(small_i[:, 1, 0:E], small_i[:, 0, 0:E], 7, None, ALU.arith_shift_right).then_inc(s("tiles"), 1)
                dve.wait_ge(s("tiles"), 2)
                dve.tensor_copy(sm(1), small_i[:, 1, 0:E]).then_inc(s("tiles"), 1)
                dve.memset(sm(0), 1.0).then_inc(s("tiles"), 1)
                dve.wait_ge(s("tiles"), 4)
                dve.tensor_tensor_scan(sm(2), sm(0), sm(1), 0.0, ALU.mult, ALU.add).then_inc(s("tiles"), 1)
                dve.wait_ge(s("tiles"), 5)
                dve.tensor_tensor(sm(3), sm(2), sm(1), ALU.subtract).then_inc(s("tiles"), 1)
                dve.wait_ge(s("tiles"), 6)
                dve.tensor_scalar(sm(4), sm(3), float(P), None, ALU.mult).then_inc(s("tiles"), 1)
                dve.tensor_tensor(cmp_, sm(2).unsqueeze(1).broadcast_to([P, NC, E]),
                                  const("slot_id").unsqueeze(2).broadcast_to([P, NC, E]), ALU.is_le).then_inc(s("cmp"), 1)
                dve.wait_ge(s("cmp"), 1)
                dve.tensor_reduce(small[:, 5, 0:NC], cmp_, AX.X, ALU.add).then_inc(s("cmp"), 1)
                dve.wait_ge(s("cmp"), 2)
                dve.tensor_scalar(expert_of[:], small[:, 5, 0:NC], float(E - 1), None, ALU.min).then_inc(s("expert_of"), 1)
                dve.wait_ge(s("expert_turned"), 1)
                dve.tensor_scalar(expert_row[:], PS[0][0:1, 0:NC * P], float(row_scale), None, ALU.mult).then_inc(s("expert_row"), 1)
                dve.wait_ge(s("tiles"), 7)
                dve.tensor_tensor(running, running, counts, ALU.subtract).then_inc(s("place"), 1)
                dve.wait_ge(s("place"), 1)
                dve.tensor_tensor(running, running, sm(4).unsqueeze(2).broadcast_to([P, E, TILES]), ALU.add).then_inc(s("place"), 1)
                dve.wait_ge(s("place"), 2)
                dve.tensor_tensor(position, position, running.rearrange("p e t -> p t e"), ALU.add).then_inc(s("place"), 1)
                dve.wait_ge(s("place"), 3)
                for k in range(K):
                    if k:
                        dve.wait_ge(s("placef"), k)
                    dve.tensor_tensor(picked, position, hot[:, k, :, :], ALU.mult).then_inc(s("picked"), 1)
                    dve.wait_ge(s("picked"), k + 1)
                    dve.tensor_reduce(placef[:, k, :], picked, AX.X, ALU.add).then_inc(s("placef"), 1)
                dve.wait_ge(s("placef"), K)
                for k in range(K):
                    dve.tensor_copy(place[k][:], placef[:, k, :]).then_inc(s("places"), 1)
                if gates_dve is not None:
                    gates_dve(dve, s)

            def sp_prog(sp):
                if L == 0:
                    sp.wait_ge(sem("plain_in"), 16 * len(plain))
                    sp.wait_ge(sem("slots_cleared"), n_cleared)

            stage(pe_prog, act_prog, dve_prog, None, sp_prog)
            return place, expert_row

        layer_norm(0, True)
        logits0 = arena[:, 13824:13824 + TILES * E0].rearrange("p (t e) -> p t e", e=E0)
        top8_0 = sb("top8_0", [P, TILES, 8])
        gates0 = sb("gates0", [P, TILES, 8])

        def gates0_act(act, s):
            act.wait_ge(s("top8"), TILES)
            act.activation(gates0[:], top8_0[:], ACT.Sigmoid).then_inc(s("gates"), 1)

        place0, expert_row0 = routing(0, E0, K0, WT["sel"], None, S0, Xs0, logits0, top8_0, gates0_act, 1, arena)

        silu_h, gated = work[:, 0:2 * T].rearrange("p (r n) -> p r n", r=2), work[:, 2048:2048 + 2 * T].rearrange("p (r n) -> p r n", r=2)
        miss = work[:, 4096:4096 + T]
        miss2 = work[:, 5120:5120 + T]
        scale_d = sb("scale_d", [P, 2])
        loss_p = sb("loss_p", [P, 1])
        decay_step = sb("decay_step", [P, 1])

        def chunk(buf, c):
            return buf[:].rearrange("p (b c k) -> p b c k", b=B, c=NCH)[:, :, c, :]

        def as_chunk(ap):
            return ap.rearrange("p (b k) -> p b k", b=B)

        def fast_pe(pe):
            def up(c, f):
                n = c * FC + f
                if n >= 2:
                    pe.wait_ge(sem("silu"), n - 1)
                pe.matmul(PS[n % 2][:], W0[:, f * P:(f + 1) * P], chunk(xn, c), start=True, stop=True).then_inc(sem("h0"), 1)
                if n >= 2:
                    pe.wait_ge(sem("gated"), n - 1)
                pe.matmul(PS[2 + n % 2][:], W2[:, f * P:(f + 1) * P], chunk(xn, c), start=True, stop=True).then_inc(sem("h2"), 1)

            def down(c, f):
                n = c * FC + f
                pe.wait_ge(sem("gated"), n + 1)
                if f == 0 and c >= 1:
                    pe.wait_ge(sem("fast_added"), c)
                m = pe.matmul(PS[4][:], W1[:, f, :], gated[:, n % 2, :], start=(f == 0), stop=(f == FC - 1))
                m.then_inc(sem("down"), 1)

            for c in range(NCH):
                if c == 0:
                    up(c, 0)
                for f in range(FC):
                    if f < FC - 1:
                        up(c, f + 1)
                    elif c < NCH - 1:
                        up(c + 1, 0)
                    down(c, f)
                pe.wait_ge(sem("loss_p"), c + 1)
                if c >= 1:
                    pe.wait_ge(sem("decay_step"), c)
                pe.matmul(PS[5][:, 0:1], ones_loss[:], loss_p[:], start=True, stop=True).then_inc(sem("loss"), 1)

        def fast_act(act):
            for c in range(NCH):
                for f in range(FC):
                    n = c * FC + f
                    act.wait_ge(sem("h0"), n + 1)
                    act.wait_ge(sem("scale_d"), 1 + 2 * c)
                    if n >= 2:
                        act.wait_ge(sem("gated"), n - 1)
                    act.activation(silu_h[:, n % 2, :], PS[n % 2][:], ACT.Silu, scale=scale_d[:, 0:1]).then_inc(sem("silu"), 1)
                act.wait_ge(sem("miss"), c + 1)
                act.activation(miss2, miss, ACT.Square, accum_out=loss_p[:]).then_inc(sem("loss_p"), 1)

        def fast_dve(dve):
            dve.memset(scale_d[:], 1.0).then_inc(sem("scale_d"), 1)
            for c in range(NCH):
                for f in range(FC):
                    n = c * FC + f
                    dve.wait_ge(sem("silu"), n + 1)
                    dve.wait_ge(sem("h2"), n + 1)
                    if n >= 2:
                        dve.wait_ge(sem("down"), n - 1)
                    dve.tensor_tensor(gated[:, n % 2, :], silu_h[:, n % 2, :], PS[2 + n % 2][:], ALU.mult).then_inc(sem("gated"), 1)
                dve.wait_ge(sem("down"), FC * (c + 1))
                dve.wait_ge(sem("scale_d"), 1 + 2 * c)
                if c:
                    dve.wait_ge(sem("loss_p"), c)
                o = as_chunk(PS[4][:])
                dve.scalar_tensor_tensor(as_chunk(miss), o, scale_d[:, 1:2], chunk(xn, c), ALU.mult, ALU.subtract).then_inc(sem("miss"), 1)
                dve.scalar_tensor_tensor(chunk(xT, c), o, scale_d[:, 1:2], chunk(xT, c), ALU.mult, ALU.add).then_inc(sem("fast_added"), 1)
                dve.wait_ge(sem("loss"), c + 1)
                dve.tensor_scalar(decay_step[:], PS[5][:, 0:1], -LR, 1.0, ALU.mult, ALU.add).then_inc(sem("decay_step"), 1)
                dve.wait_ge(sem("decay_step"), c + 1)
                dve.wait_ge(sem("fast_added"), c + 1)
                dve.tensor_tensor(scale_d[:, 0:1], scale_d[:, 0:1], decay_step[:], ALU.mult).then_inc(sem("scale_d"), 1)
                dve.wait_ge(sem("scale_d"), 2 + 2 * c)
                dve.tensor_tensor(scale_d[:, 1:2], scale_d[:, 0:1], scale_d[:, 0:1], ALU.mult).then_inc(sem("scale_d"), 1)

        def sort_pool(L, K, Xs, place):
            def pool_prog(pool):
                for t in range(TILES):
                    for k in range(K):
                        pool.indirect_dma_start(out=Xs, out_offset=bass.IndirectOffsetOnAxis(ap=place[k][:, t:t + 1], axis=0),
                                                in_=xtok[:, t, :], in_offset=None).then_inc(sem(f"sorted{L}"), 16)
                pool.wait_ge(sem(f"sorted{L}"), 16 * TILES * K)
            return pool_prog

        def experts0_load(sp):
            sp.dma_start(keys, A["L0_ffn_keys"].rearrange("e i h -> i e h")).then_inc(sem("experts0_in"), 16)
            sp.dma_start(values, A["L0_ffn_values"].rearrange("e h o -> h e o")).then_inc(sem("experts0_in"), 16)

        TBL = P + 3
        table = sb("mode_powers", [P, TBL])
        to_taps = sb("to_taps", [P, D])
        into_state = sb("into_state", [P, P])
        from_state = sb("from_state", [P, P])
        turn_state = sb("turn_state", [P, P])
        kernel_pad = nc.dram_tensor("kernel_pad", (D, 2 * P), FP32).ap()

        def tables():
            s = lambda n: sem(f"tables_{n}")
            TWO_PI = 6.2831855
            C1 = 6.28125
            C2 = float(np.float32(int((2 * np.pi - C1) * 2 ** 17) / 2.0 ** 17))
            C3 = float(np.float32(2 * np.pi - C1 - C2))
            BIG = 12582912.0
            w = lambda i: work[:, i * 256:i * 256 + TBL]
            phase, turns, rest, mag, sine = (w(i) for i in range(5))
            col = work[:, 2048:2056]
            taps = work[0:NS, 2304:2304 + D]
            dup = work[0:NS, 2560:2560 + P]
            kpad = work[:, 3072:3072 + 2 * P]
            sgn = const("imag_sign")
            chain = [0]

            def act_prog(act):
                act.activation(col[:, 1:2], decay[:], ACT.Exp).then_inc(s("rate"), 1)
                act.wait_ge(s("neg_rate"), 1)
                act.activation(mag, const("lags"), ACT.Exp, scale=col[:, 2:3]).then_inc(s("mag"), 1)
                act.wait_ge(s("reduced"), 1)
                act.activation(sine, rest, ACT.Sin).then_inc(s("sine"), 1)

            def dve_prog(dve):
                def step(m):
                    chain[0] += 1
                    m.then_inc(s("step"), 1)
                    dve.wait_ge(s("step"), chain[0])
                step(dve.memset(kpad, 0.0))
                step(dve.tensor_scalar(col[:, 0:1], freq[:], TWO_PI, None, ALU.mult))
                step(dve.tensor_scalar(phase, const("lags"), col[:, 0:1], None, ALU.mult))
                dve.wait_ge(s("rate"), 1)
                dve.tensor_scalar(col[:, 2:3], col[:, 1:2], -1.0, None, ALU.mult).then_inc(s("neg_rate"), 1)
                step(dve.tensor_scalar(turns, const("quarter"), 0.25, None, ALU.mult))
                step(dve.scalar_tensor_tensor(turns, phase, 1.0 / TWO_PI, turns, ALU.mult, ALU.add))
                step(dve.tensor_scalar(turns, turns, BIG, None, ALU.add))
                step(dve.tensor_scalar(turns, turns, -BIG, None, ALU.add))
                for c in (C1, C2, C3):
                    step(dve.scalar_tensor_tensor(phase, turns, -c, phase, ALU.mult, ALU.add))
                step(dve.scalar_tensor_tensor(rest, const("quarter"), float(np.pi / 2), phase, ALU.mult, ALU.add))
                dve.tensor_scalar(rest, rest, 3.1415925, -3.1415925, ALU.min, ALU.max).then_inc(s("reduced"), 1)
                dve.wait_ge(s("sine"), 1)
                dve.wait_ge(s("mag"), 1)
                dve.tensor_tensor(table[:], sine, mag, ALU.mult).then_inc(s("table"), 1)
                dve.tensor_tensor(taps, WT["in_proj"], out_proj[:], ALU.mult).then_inc(s("taps"), 1)
                dve.tensor_tensor(dup, ident[0:NS, :], const("swap_halves")[0:NS, :], ALU.add).then_inc(s("taps"), 1)
                dve.wait_ge(s("table"), 1)
                dve.tensor_scalar(from_state[:], table[:, 0:P], sgn, None, ALU.mult).then_inc(s("made"), 1)
                dve.tensor_tensor(col[:, 3:4], table[:, P + 2:P + 3], sgn, ALU.mult).then_inc(s("made"), 1)
                dve.wait_ge(s("made"), 2)
                dve.tensor_scalar(turn_state[:], const("swap_halves"), col[:, 3:4], None, ALU.mult).then_inc(s("made"), 1)
                dve.wait_ge(s("made"), 3)
                dve.scalar_tensor_tensor(turn_state[:], ident, table[:, P + 1:P + 2], turn_state[:], ALU.mult, ALU.add).then_inc(s("made"), 1)
                dve.wait_ge(s("products"), 3)
                dve.tensor_copy(into_state[:], PS[0][:, 0:P]).then_inc(s("made"), 1)
                dve.tensor_copy(to_taps[:], PS[1][:, 0:P]).then_inc(s("made"), 1)
                dve.tensor_copy(kpad[:, 0:P], PS[2][:, 0:P]).then_inc(s("kernel"), 1)

            def pe_prog(pe):
                pe.wait_ge(s("table"), 1)
                pe.wait_ge(s("taps"), 2)
                pe.transpose(PS[0][:, 0:P], table[:, 1:P + 1], ident).then_inc(s("products"), 1)
                pe.matmul(PS[1][:, 0:P], dup, taps, start=True, stop=True).then_inc(s("products"), 1)
                pe.matmul(PS[2][:, 0:P], taps, table[0:NS, 1:P + 1], start=True, stop=True).then_inc(s("products"), 1)

            def sp_prog(sp):
                sp.wait_ge(s("kernel"), 1)
                sp.dma_start(kernel_pad, kpad).then_inc(s("kernel_out"), 16)
                sp.wait_ge(s("kernel_out"), 16)
            return pe_prog, act_prog, dve_prog, sp_prog

        tables_pe, tables_act, tables_dve, tables_sp = tables()

        def then(first, second):
            def prog(eng):
                first(eng)
                second(eng)
            return prog

        stage(then(fast_pe, tables_pe), then(fast_act, tables_act), then(fast_dve, tables_dve),
              sort_pool(0, K0, Xs0, place0), then(experts0_load, tables_sp))

        BL = 4

        def experts(L, G, slots, Xs, Ys, row, up_w, up_bias, down_w, down_bias, loaded):
            s = lambda n: sem(f"experts_{n}")
            FB = BL // G
            NG = slots // G
            W = G * D
            blk = lambda i: work[:, i * 1024:(i + 1) * 1024].rearrange("p (r s d) -> p r s d", r=2, s=BL)
            rowsT, hidden, biased = (blk(i) for i in range(3))
            rows_out = work[:, 3840:5888].rearrange("p (r s d) -> p r s d", r=4, s=BL)
            rows_in = work[:, 5888:7936].rearrange("p (r s d) -> p r s d", r=4, s=BL)
            bias_now = work[:, 3072:3072 + 4 * BL].rearrange("p (r s) -> p r s", r=4)
            down_bias_now = work[0:1, 3200:3200 + 4 * D].rearrange("p (r d) -> p r d", r=4)
            up_now, down_now = (xtok[:, 16 * i:16 * (i + 1), :].rearrange("p (r s) d -> p r s d", r=4) for i in range(2))
            shares = {"dve": ((0, 2), (0, 2)), "act": ((2, 3), (2, 3)), "pool": ((3, 4), (3, 4))} if G == BL else \
                {"dve": ((0, 1), (0, 4)), "act": ((2, 4), (0, 0)), "pool": ((1, 2), (0, 0))}

            def slot_rows(X, n):
                return X[bass.ds(n * (G * P), G * P), :].rearrange("(s p) d -> p s d", p=P)

            U = 8
            assert NG % U == 0

            def used(n, ring):
                return not isinstance(n, int) or n >= ring

            def over_groups(eng, body):
                for r in range(U):
                    body(r, r, 0)
                with eng.Fori(1, NG // U) as i:
                    for r in range(U):
                        body(i * U + r, r, i)

            def expert_of_slot(eng, n, j):
                return eng.value_load(row[0:1, bass.ds(n * G + j, 1)], min_val=0, max_val=(E0 if L == 0 else E2) - 1)

            def copy_share(eng, copy, who, n, r):
                if used(n, 4):
                    eng.wait_ge(s("down"), n - 3)
                    if up_bias is not None:
                        eng.wait_ge(s("biased"), n - 3)
                for j in range(G):
                    e = None
                    for (first, end), weights, now in zip(shares[who], (up_w, down_w), (up_now, down_now)):
                        a, b = max(first, j * FB), min(end, (j + 1) * FB)
                        if a < b:
                            if e is None:
                                e = expert_of_slot(eng, n, j)
                            last = copy(now[:, r % 4, a:b, :].rearrange("p f d -> p (f d)"),
                                        weights[:, bass.ds(e * (FB * D) + (a - j * FB) * D, (b - a) * D)])
                    if e is not None and who == "dve" and down_bias is not None:
                        last = copy(down_bias_now[0:1, r % 4, :], down_bias[0:1, bass.ds(e * D, D)])
                    if e is not None and who == "pool" and up_bias is not None:
                        last = copy(bias_now[:, r % 4, :], up_bias[:, bass.ds(e * FB, FB)])
                last.then_inc(s(f"weights_{who}"), 1)

            def sp_prog(sp):
                def store(n, r):
                    sp.wait_ge(s("rows_out"), n + 1)
                    sp.dma_start(slot_rows(Ys, n), rows_out[:, r % 4, 0:G, :]).then_inc(s(f"stored{r % 4}"), 16)

                def step(n, r, i):
                    if used(n, 4):
                        sp.wait_ge(s("rows_turned"), n - 3)
                    sp.dma_start(rows_in[:, r % 4, 0:G, :], slot_rows(Xs, n)).then_inc(s(f"rows_in{r % 4}"), 16)
                    if used(n, 4):
                        store(n - 4, (r - 4) % U)
                over_groups(sp, step)
                for n in range(NG - 4, NG):
                    store(n, n % U)
                for r in range(4):
                    sp.wait_ge(s(f"stored{r}"), 16 * (NG // 4))

            def pool_prog(pool):
                pool.wait_ge(sem(f"experts{L}_in"), loaded)
                over_groups(pool, lambda n, r, i: copy_share(pool, pool.tensor_copy, "pool", n, r))

            def pe_prog(pe):
                def turn(n, r, i):
                    pe.wait_ge(s(f"rows_in{r % 4}"), i * (16 * U // 4) + 16 * (r // 4 + 1))
                    if used(n, 2):
                        pe.wait_ge(s("rowsT"), n - 1)
                    for j in range(G):
                        last = pe.transpose(PS[r % 2][:, j * P:(j + 1) * P], rows_in[:, r % 4, j, :], ident)
                    last.then_inc(s("rows_turned"), 1)

                def up(n, r):
                    pe.wait_ge(s("rowsT"), n + 1)
                    for who in shares:
                        pe.wait_ge(s(f"weights_{who}"), n + 1)
                    if used(n, 2):
                        pe.wait_ge(s("biased" if up_bias is not None else "hidden"), n - 1)
                    for q in range(BL):
                        last = pe.matmul(PS[2 + r % 2][:, q * P:(q + 1) * P], up_now[:, r % 4, q, :], rowsT[:, r % 2, q // FB, :],
                                         start=True, stop=True)
                    last.then_inc(s("up"), 1)

                def down(n, r):
                    pe.wait_ge(s("hidden"), n + 1)
                    if used(n, 2):
                        pe.wait_ge(s("rows_out"), n - 1)
                    for j in range(G):
                        dst = PS[4 + r % 2][:, j * P:(j + 1) * P]
                        for f in range(FB):
                            last = pe.matmul(dst, hidden[:, r % 2, j * FB + f, :], down_now[:, r % 4, j * FB + f, :],
                                             start=(f == 0), stop=(f == FB - 1 and down_bias is None))
                        if down_bias is not None:
                            last = pe.matmul(dst, one_row[:], down_bias_now[0:1, r % 4, :], start=False, stop=True)
                    last.then_inc(s("down"), 1)

                def step(n, r, i):
                    turn(n, r, i)
                    if used(n, 1):
                        up(n - 1, (r - 1) % U)
                    if used(n, 2):
                        down(n - 2, (r - 2) % U)
                over_groups(pe, step)
                up(NG - 1, U - 1)
                down(NG - 2, U - 2)
                down(NG - 1, U - 1)

            def act_prog(act):
                def rowsT_copy(n, r):
                    act.wait_ge(s("rows_turned"), n + 1)
                    if used(n, 2):
                        act.wait_ge(s("up"), n - 1)
                    act.activation(rowsT[:, r % 2, 0:G, :], PS[r % 2][:, 0:W].rearrange("p (s d) -> p s d", s=G), ACT.Copy).then_inc(s("rowsT"), 1)

                def out_copy(n, r, stored_before):
                    act.wait_ge(s("down"), n + 1)
                    if stored_before is not None:
                        act.wait_ge(s(f"stored{r % 4}"), stored_before)
                    act.activation(rows_out[:, r % 4, 0:G, :], PS[4 + r % 2][:, 0:W].rearrange("p (s d) -> p s d", s=G), ACT.Copy).then_inc(s("rows_out"), 1)

                act.wait_ge(sem(f"experts{L}_in"), loaded)

                def step(n, r, i):
                    rowsT_copy(n, r)
                    copy_share(act, lambda o, v: act.activation(o, v, ACT.Copy), "act", n, r)
                    if used(n, 2):
                        before = i * (16 * U // 4) + 16 * ((r - 2) // 4)
                        out_copy(n - 2, (r - 2) % U, before if used(n, 6) else None)
                over_groups(act, step)
                out_copy(NG - 2, U - 2, 16 * (NG // 4 - 1))
                out_copy(NG - 1, U - 1, 16 * (NG // 4 - 1))

            def dve_prog(dve):
                dve.wait_ge(sem(f"experts{L}_in"), loaded)

                def relu(n, r):
                    dve.wait_ge(s("up"), n + 1)
                    src = PS[2 + r % 2][:].rearrange("p (s d) -> p s d", s=BL)
                    if used(n, 2):
                        dve.wait_ge(s("down"), n - 1)
                    if up_bias is not None:
                        dve.wait_ge(s("weights_pool"), n + 1)
                        dve.tensor_tensor(biased[:, r % 2, :, :], src, bias_now[:, r % 4, :].unsqueeze(2).broadcast_to([P, BL, D]), ALU.add).then_inc(s("biased"), 1)
                        dve.wait_ge(s("biased"), n + 1)
                        src = biased[:, r % 2, :, :]
                    dve.tensor_scalar(hidden[:, r % 2, :, :], src, 0.0, None, ALU.max).then_inc(s("hidden"), 1)

                def step(n, r, i):
                    copy_share(dve, dve.tensor_copy, "dve", n, r)
                    if used(n, 1):
                        relu(n - 1, (r - 1) % U)
                over_groups(dve, step)
                relu(NG - 1, U - 1)

            stage(pe_prog, act_prog, dve_prog, pool_prog, sp_prog)

        one_row = sb("one_row", [1, P])
        experts(0, 4, S0, Xs0, Ys0, expert_row0, arena[:, 0:E0 * D], None, arena[:, E0 * D:2 * E0 * D], None, 32)

        def combine(L, K, Ys, place, gate):
            s = lambda n: sem(f"combine_{n}")
            R = 4
            got = work[:, 0:R * K * D].rearrange("p (r k d) -> p r k d", r=R, k=K)
            summed = work[:, 4096:4096 + 2 * TPB * D].rearrange("p (r t d) -> p r t d", r=2, t=TPB)

            def pool_prog(pool):
                for t in range(TILES):
                    if t >= R:
                        pool.wait_ge(s("tile"), t - R + 1)
                    for k in range(K):
                        pool.indirect_dma_start(out=got[:, t % R, k, :], out_offset=None, in_=Ys,
                                                in_offset=bass.IndirectOffsetOnAxis(ap=place[k][:, t:t + 1], axis=0)).then_inc(sem(f"got{L}_{t % R}"), 16)

            def dve_prog(dve):
                for t in range(TILES):
                    b, j = divmod(t, TPB)
                    dve.wait_ge(sem(f"got{L}_{t % R}"), 16 * K * (t // R + 1))
                    if j == 0 and b >= 2:
                        dve.wait_ge(s("turned"), b - 1)
                    to = summed[:, b % 2, j, :]
                    for k in range(K):
                        if k == 0:
                            m = dve.tensor_scalar(to, got[:, t % R, k, :], gate(t, k), None, ALU.mult)
                        else:
                            m = dve.scalar_tensor_tensor(to, got[:, t % R, k, :], gate(t, k), to, ALU.mult, ALU.add)
                        if k < K - 1:
                            m.then_inc(s("part"), 1)
                            dve.wait_ge(s("part"), t * (K - 1) + k + 1)
                    m.then_inc(s("tile"), 1)
                    if j == TPB - 1 and b >= 1:
                        add(dve, b - 1)
                add(dve, B - 1)

            def add(dve, b):
                dve.wait_ge(s("turned"), b + 1)
                dve.tensor_tensor(cols(xT, b), cols(xT, b), PS[b % 2][:], ALU.add).then_inc(s("added"), 1)

            def pe_prog(pe):
                for b in range(B):
                    pe.wait_ge(s("tile"), TPB * (b + 1))
                    if b >= 2:
                        pe.wait_ge(s("added"), b - 1)
                    for j in range(TPB):
                        last = pe.transpose(PS[b % 2][:, j * P:(j + 1) * P], summed[:, b % 2, j, :], ident)
                    last.then_inc(s("turned"), 1)

            stage(pe_prog, None, dve_prog, pool_prog)

        def layer1():
            s = lambda n: sem(f"l1_{n}")
            off = [0]

            def take(n):
                off[0] += n
                assert off[0] <= 16384
                return arena[:, off[0] - n:off[0]]
            QW = 3 * D + 1
            R = 4
            qkv = take(2 * TPB * QW).rearrange("p (r t c) -> p r t c", r=2, t=TPB)
            qk = lambda r: qkv[:, r, :, 0:2 * D]
            sq = take(TPB * 2 * D).rearrange("p (t c) -> p t c", t=TPB)
            table_c = take(TPB * 2 * D).rearrange("p (t c) -> p t c", t=TPB)
            table_s = take(TPB * 2 * D).rearrange("p (t c) -> p t c", t=TPB)
            normed = take(TPB * 2 * D).rearrange("p (t c) -> p t c", t=TPB)
            part_c = take(TPB * 2 * D).rearrange("p (t c) -> p t c", t=TPB)
            part_s = take(TPB * 2 * D).rearrange("p (t c) -> p t c", t=TPB)
            kf = take(TPB * D).rearrange("p (t c) -> p t c", t=TPB)
            qT = take(T)
            VW = D + H
            kv = take(VW)
            attn = take(T).rearrange("p (t c) -> p t c", t=TPB)
            squared = take(T)
            ms, dev, inv, ln_inv, y_inv = take(8), take(8), take(8), take(TPB), take(TPB)
            den = take(TPB * H)
            one_minus = take(2)
            xr, xk, r_gate, k_relu, k_sq, mixed, attnT, y, y2, y_scaled = (work[:, i * T:(i + 1) * T] for i in range(10))
            got = work[:, 10 * T:10 * T + R * K0 * D].rearrange("p (r k d) -> p r k d", r=R, k=K0)
            summed = work[:, 14 * T:16 * T].rearrange("p (r t d) -> p r t d", r=2, t=TPB)
            Q3 = turnedT[:, 0:3 * P]

            def pe_prog(pe):
                def project_qkv(b):
                    pe.wait_ge(s("xn"), b + 1)
                    for t in range(TPB):
                        n = b * TPB + t
                        if n >= 2:
                            pe.wait_ge(s("qkv_sb"), n - 1)
                        c = b * T + t * P
                        pe.matmul(PS[n % 2][:, 0:3 * D], xn[:, c:c + P], Q3, start=True, stop=True).then_inc(s("qkv"), 1)

                def key(b):
                    pe.wait_ge(s("xk"), b + 1)
                    if b:
                        pe.wait_ge(s("mixed"), b)
                    pe.matmul(PS[6][:], WT["k"], xk, start=True, stop=True).then_inc(s("k"), 1)

                def receptance(b):
                    pe.wait_ge(s("xr"), b + 1)
                    pe.wait_ge(s("k_relu"), b + 1)
                    pe.matmul(PS[6][:], WT["r"], xr, start=True, stop=True).then_inc(s("r"), 1)

                def value(b):
                    pe.wait_ge(s("k_sq"), b + 1)
                    pe.wait_ge(s("r_gate"), b + 1)
                    pe.matmul(PS[6][:], WT["v"], k_sq, start=True, stop=True).then_inc(s("v"), 1)

                def turn_attention(b):
                    pe.wait_ge(s("attn"), 2 * (b + 1))
                    if b:
                        pe.wait_ge(s("y_scaled"), b)
                    for t in range(TPB):
                        last = pe.transpose(PS[2][:, t * P:(t + 1) * P], attn[:, t, :], ident)
                    last.then_inc(s("attn_turned"), 1)

                def project_out(b):
                    pe.wait_ge(s("attnT"), b + 1)
                    pe.wait_ge(s("kv_sb"), 2 * (b + 1))
                    pe.matmul(PS[3][:], WT["out1"], attnT, start=True, stop=True).then_inc(s("projected"), 1)

                def y_mean_squares(b):
                    pe.wait_ge(s("y2"), b + 1)
                    for t in range(TPB):
                        last = pe.matmul(PS[2][:, t:t + 1], y2[:, t * P:(t + 1) * P], ones_mean[:, 0:1], start=True, stop=True)
                    last.then_inc(s("y_ms"), 1)

                def y_spread(b):
                    pe.wait_ge(s("y_inv"), b + 1)
                    if b + 1 < B:
                        pe.wait_ge(s("qT"), b + 2)
                    for t in range(TPB):
                        last = pe.matmul(PS[2][:, t * P:(t + 1) * P], y_inv[:, t:t + 1].broadcast_to([P, P]), ident, start=True, stop=True)
                    last.then_inc(s("y_spread"), 1)

                def turn_rows(b):
                    pe.wait_ge(s("tile"), TPB * (b + 1))
                    if b:
                        pe.wait_ge(s("xn"), b)
                    for j in range(TPB):
                        last = pe.transpose(PS[7][:, j * P:(j + 1) * P], summed[:, b % 2, j, :], ident)
                    last.then_inc(s("turned"), 1)

                def mean(b):
                    pe.wait_ge(s("added"), b + 1)
                    pe.matmul(PS[7][:], ones_mean[:], cols(xT, b), start=True, stop=True).then_inc(s("mean"), 1)

                def variance(b):
                    pe.wait_ge(s("squared"), b + 1)
                    for t in range(TPB):
                        last = pe.matmul(PS[7][:, t:t + 1], squared[:, t * P:(t + 1) * P], ones_mean[:, 0:1], start=True, stop=True)
                    last.then_inc(s("var"), 1)

                def ln_spread(b):
                    pe.wait_ge(s("ln_inv"), b + 1)
                    for t in range(TPB):
                        last = pe.matmul(PS[7][:, t * P:(t + 1) * P], ln_inv[:, t:t + 1].broadcast_to([P, P]), ident, start=True, stop=True)
                    last.then_inc(s("ln_spread"), 1)

                def turn_queries(b):
                    pe.wait_ge(s("rotated"), b + 1)
                    if b:
                        pe.wait_ge(s("y_dev"), b)
                    for t in range(TPB):
                        last = pe.transpose(PS[2][:, t * P:(t + 1) * P], part_c[:, t, 0:D], ident)
                    last.then_inc(s("q_turned"), 1)

                def keys_times_values(b):
                    pe.wait_ge(s("kf"), b + 1)
                    if b:
                        pe.wait_ge(s("y"), b)
                    for t in range(TPB):
                        last = pe.matmul(PS[3][:, 0:D + 1], kf[:, t, :], qkv[:, b % 2, t, 2 * D:QW], start=(t == 0), stop=(t == TPB - 1))
                    last.then_inc(s("kv"), 1)

                def attend(b):
                    pe.wait_ge(s("qT"), b + 1)
                    pe.wait_ge(s("kv_sb"), 2 * (b + 1))
                    if b:
                        pe.wait_ge(s("attn"), 2 * b)
                    for t in range(TPB):
                        last = pe.matmul(PS[4 + t // 2][:, (t % 2) * VW:(t % 2 + 1) * VW], qT[:, t * P:(t + 1) * P], kv, start=True, stop=True)
                    last.then_inc(s("res"), 1)

                for i in range(-1, B + 1):
                    now, before, after = 0 <= i < B, i >= 1, i + 1 < B
                    if before:
                        turn_attention(i - 1)
                    if now:
                        project_qkv(i)
                    if before:
                        project_out(i - 1)
                    if now:
                        key(i)
                    if before:
                        y_mean_squares(i - 1)
                    if now:
                        receptance(i)
                    if after:
                        turn_rows(i + 1)
                        mean(i + 1)
                    if now:
                        value(i)
                    if after:
                        variance(i + 1)
                    if now:
                        turn_queries(i)
                        keys_times_values(i)
                    if after:
                        ln_spread(i + 1)
                    if before:
                        y_spread(i - 1)
                    if now:
                        attend(i)

            def act_prog(act):
                def copy_attention(b):
                    act.wait_ge(s("attn_turned"), b + 1)
                    if b:
                        act.wait_ge(s("projected"), b)
                    act.activation(attnT, PS[2][:], ACT.Copy).then_inc(s("attnT"), 1)

                def own_part(b):
                    act.wait_ge(s("xn"), b + 1)
                    for to, m, name, used in ((xk, "L1_ffn_mu_k", "xk_part", "k"), (xr, "L1_ffn_mu_r", "xr_part", "r")):
                        if b:
                            act.wait_ge(s(used), b)
                        act.activation(to, cols(xn, b), ACT.Copy, scale=vec[m]).then_inc(s(name), 1)

                def square_qk(b):
                    act.wait_ge(s("qkv_sb"), TPB * (b + 1))
                    if b:
                        act.wait_ge(s("ms"), b)
                    act.activation(sq, qk(b % 2), ACT.Square).then_inc(s("sq"), 1)

                def project_bias(b):
                    act.wait_ge(s("projected"), b + 1)
                    if b:
                        act.wait_ge(s("y_scaled"), b)
                        act.wait_ge(s("y_ms"), b)
                    act.activation(y2, PS[3][:], ACT.Square, bias=vec["L1_attn_bout"]).then_inc(s("y2"), 1)
                    act.activation(y, PS[3][:], ACT.Identity, bias=vec["L1_attn_bout"]).then_inc(s("y"), 1)

                def receptance_and_key(b):
                    act.wait_ge(s("k"), b + 1)
                    act.activation(k_relu, PS[6][:], ACT.Relu).then_inc(s("k_relu"), 1)
                    act.wait_ge(s("k_relu"), b + 1)
                    if b:
                        act.wait_ge(s("v"), b)
                    act.activation(k_sq, k_relu, ACT.Square).then_inc(s("k_sq"), 1)
                    act.wait_ge(s("r"), b + 1)
                    if b:
                        act.wait_ge(s("mixed"), b)
                    act.activation(r_gate, PS[6][:], ACT.Sigmoid).then_inc(s("r_gate"), 1)

                def qk_deviation(b):
                    act.wait_ge(s("ms"), b + 1)
                    act.activation(dev, ms, ACT.Sqrt, bias=eps_r1[:], scale=1.0 / D).then_inc(s("dev"), 1)

                def y_deviation(b):
                    act.wait_ge(s("y_ms"), b + 1)
                    if b:
                        act.wait_ge(s("y_spread"), b)
                    act.activation(y_inv, PS[2][:, 0:TPB], ACT.Sqrt, bias=eps_r1[:]).then_inc(s("y_dev"), 1)

                def square(b):
                    act.wait_ge(s("centred"), b + 1)
                    if b:
                        act.wait_ge(s("var"), b)
                    act.activation(squared, cols(xn, b), ACT.Square).then_inc(s("squared"), 1)

                def ln_deviation(b):
                    act.wait_ge(s("var"), b + 1)
                    if b:
                        act.wait_ge(s("ln_spread"), b)
                    act.activation(ln_inv, PS[7][:, 0:TPB], ACT.Sqrt, bias=eps_ln[:]).then_inc(s("ln_dev"), 1)

                def keys(b):
                    act.wait_ge(s("rotated"), b + 1)
                    if b:
                        act.wait_ge(s("kv"), b)
                    act.activation(kf, part_c[:, :, D:2 * D], ACT.Relu).then_inc(s("kf"), 1)

                def queries(b):
                    act.wait_ge(s("q_turned"), b + 1)
                    if b:
                        act.wait_ge(s("res"), b)
                    act.activation(qT, PS[2][:], ACT.Relu).then_inc(s("qT"), 1)

                for i in range(-1, B + 1):
                    now, before, after = 0 <= i < B, i >= 1, i + 1 < B
                    if before:
                        copy_attention(i - 1)
                    if now:
                        own_part(i)
                        square_qk(i)
                    if before:
                        project_bias(i - 1)
                    if now:
                        receptance_and_key(i)
                        qk_deviation(i)
                    if before:
                        y_deviation(i - 1)
                    if after:
                        square(i + 1)
                    if now:
                        keys(i)
                    if after:
                        ln_deviation(i + 1)
                    if now:
                        queries(i)

            def dve_prog(dve):
                dve.memset(qkv[:, :, :, 3 * D:QW], 1.0).then_inc(s("prep"), 1)
                for i, g in enumerate(("L1_attn_gq", "L1_attn_gk")):
                    grow = rows[g][:].rearrange("p (h w) -> p h w", w=HD)
                    gswap = rows[g][:].rearrange("p (h w two) -> p h w two", w=HD // 2, two=2)[:, :, :, ::-1]
                    for t in range(TPB):
                        c = const("rope_cos")[:, t * HD:(t + 1) * HD].unsqueeze(1).broadcast_to([P, H, HD])
                        n = const("rope_sin")[:, t * HD:(t + 1) * HD].rearrange("p (w two) -> p w two", two=2).unsqueeze(1).broadcast_to([P, H, HD // 2, 2])
                        dve.tensor_tensor(table_c[:, t, i * D:(i + 1) * D].rearrange("p (h w) -> p h w", w=HD), grow, c, ALU.mult).then_inc(s("prep"), 1)
                        dve.tensor_tensor(table_s[:, t, i * D:(i + 1) * D].rearrange("p (h w two) -> p h w two", w=HD // 2, two=2), gswap, n, ALU.mult).then_inc(s("prep"), 1)
                for i, m in enumerate(("L1_ffn_mu_r", "L1_ffn_mu_k")):
                    dve.tensor_scalar(one_minus[:, i:i + 1], vec[m], -1.0, 1.0, ALU.mult, ALU.add).then_inc(s("prep"), 1)
                dve.wait_ge(s("prep"), 1 + 4 * TPB + 2)

                def qkv_bias(b, tiles):
                    for t in tiles:
                        n = b * TPB + t
                        dve.wait_ge(s("qkv"), n + 1)
                        if b >= 2 and t == 0:
                            dve.wait_ge(s("kv"), b - 1)
                        dve.tensor_tensor(qkv[:, b % 2, t, 0:3 * D], PS[n % 2][:, 0:3 * D], rows["L1_attn_bqkv"][:], ALU.add).then_inc(s("qkv_sb"), 1)

                def mixes(b):
                    dve.wait_ge(s("xn"), b + 1)
                    for i, to, name in ((1, xk, "xk"), (0, xr, "xr")):
                        dve.wait_ge(s(name + "_part"), b + 1)
                        dve.scalar_tensor_tensor(to[:, 1:T], xn[:, b * T:(b + 1) * T - 1], one_minus[:, i:i + 1], to[:, 1:T],
                                                 ALU.mult, ALU.add).then_inc(s(name), 1)

                def gate_rows(b):
                    for first in range(0, TPB, 2):
                        for k in range(K0):
                            for j in (first, first + 1):
                                t = b * TPB + j
                                if k == 0:
                                    dve.wait_ge(sem(f"got0_{t % R}"), 16 * K0 * (t // R + 1))
                                if k == 0 and j == 0 and b >= 2:
                                    dve.wait_ge(s("turned"), b - 1)
                                to, g = summed[:, b % 2, j, :], gates0[:, t, k:k + 1]
                                if k == 0:
                                    m = dve.tensor_scalar(to, got[:, t % R, k, :], g, None, ALU.mult)
                                else:
                                    dve.wait_ge(s("part"), (b * TPB + first) * (K0 - 1) + 2 * (k - 1) + j - first + 1)
                                    m = dve.scalar_tensor_tensor(to, got[:, t % R, k, :], g, to, ALU.mult, ALU.add)
                                m.then_inc(s("part" if k < K0 - 1 else "tile"), 1)

                def add_rows(b):
                    dve.wait_ge(s("turned"), b + 1)
                    dve.tensor_tensor(cols(xT, b), cols(xT, b), PS[7][:], ALU.add).then_inc(s("added"), 1)

                def centre(b):
                    dve.wait_ge(s("mean"), b + 1)
                    dve.tensor_tensor(cols(xn, b), cols(xT, b), PS[7][:], ALU.subtract).then_inc(s("centred"), 1)

                def invert_deviation(b):
                    dve.wait_ge(s("ln_dev"), b + 1)
                    dve.reciprocal(ln_inv, ln_inv).then_inc(s("ln_inv"), 1)

                def normalise(b):
                    dve.wait_ge(s("ln_spread"), b + 1)
                    dve.tensor_tensor(cols(xn, b), cols(xn, b), PS[7][:], ALU.mult).then_inc(s("xn"), 1)

                def mean_squares(b):
                    dve.wait_ge(s("sq"), b + 1)
                    if b:
                        dve.wait_ge(s("dev"), b)
                    dve.tensor_reduce(ms, sq.rearrange("p t (i c) -> p (t i) c", i=2), AX.X, ALU.add).then_inc(s("ms"), 1)

                def norm_qk(b):
                    dve.wait_ge(s("dev"), b + 1)
                    dve.reciprocal(inv, dev).then_inc(s("inv"), 1)
                    dve.wait_ge(s("inv"), b + 1)
                    if b:
                        dve.wait_ge(s("part_s"), b)
                    dve.tensor_tensor(normed.rearrange("p t (i c) -> p t i c", i=2), qk(b % 2).rearrange("p t (i c) -> p t i c", i=2),
                                      inv.rearrange("p (t i) -> p t i", i=2).unsqueeze(3).broadcast_to([P, TPB, 2, D]), ALU.mult).then_inc(s("normed"), 1)

                def turn_parts(b):
                    dve.wait_ge(s("normed"), b + 1)
                    if b:
                        dve.wait_ge(s("kf"), b)
                        dve.wait_ge(s("q_turned"), b)
                    dve.tensor_tensor(part_c, normed, table_c, ALU.mult).then_inc(s("part_c"), 1)

                def rotate(b):
                    dve.wait_ge(s("part_c"), b + 1)
                    dve.wait_ge(s("part_s"), b + 1)
                    dve.tensor_tensor(part_c, part_c, part_s, ALU.add).then_inc(s("rotated"), 1)

                def mix_into_x(b):
                    dve.wait_ge(s("v"), b + 1)
                    dve.wait_ge(s("r_gate"), b + 1)
                    dve.tensor_tensor(mixed, r_gate, PS[6][:], ALU.mult).then_inc(s("mixed"), 1)
                    dve.wait_ge(s("mixed"), b + 1)
                    dve.tensor_tensor(cols(xT, b), cols(xT, b), mixed, ALU.add).then_inc(s("mix_added"), 1)

                def own_heads(b):
                    dve.wait_ge(s("kv"), b + 1)
                    if b:
                        dve.wait_ge(s("res"), b)
                    dve.tensor_tensor(kv[:, 0:D], PS[3][:, 0:D], const("headblock"), ALU.mult).then_inc(s("kv_sb"), 1)
                    dve.tensor_tensor(kv[:, D:VW], const("headblock")[:, ::HD], PS[3][:, D:D + 1].broadcast_to([P, H]), ALU.mult).then_inc(s("kv_sb"), 1)

                def divide(b):
                    dve.wait_ge(s("res"), b + 1)
                    if b:
                        dve.wait_ge(s("attn_turned"), b)
                    for i in range(2):
                        both = PS[4 + i][:, 0:2 * VW].rearrange("p (t c) -> p t c", c=VW)
                        dve.tensor_scalar(den[:, i * 2 * H:(i + 1) * 2 * H].rearrange("p (t h) -> p t h", h=H), both[:, :, D:VW], EPS_LIN, None, ALU.add).then_inc(s("den"), 1)
                    dve.wait_ge(s("den"), 3 * b + 2)
                    dve.reciprocal(den, den).then_inc(s("den"), 1)
                    dve.wait_ge(s("den"), 3 * b + 3)
                    for i in range(2):
                        both = PS[4 + i][:, 0:2 * VW].rearrange("p (t c) -> p t c", c=VW)
                        dve.tensor_tensor(attn[:, 2 * i:2 * i + 2, :].rearrange("p t (h w) -> p t h w", w=HD),
                                          both[:, :, 0:D].rearrange("p t (h w) -> p t h w", w=HD),
                                          den[:, i * 2 * H:(i + 1) * 2 * H].rearrange("p (t h) -> p t h", h=H).unsqueeze(3).broadcast_to([P, 2, H, HD]),
                                          ALU.mult).then_inc(s("attn"), 1)

                def invert_y(b):
                    dve.wait_ge(s("y_dev"), b + 1)
                    dve.reciprocal(y_inv, y_inv).then_inc(s("y_inv"), 1)

                def project_into_x(b):
                    dve.wait_ge(s("y_spread"), b + 1)
                    dve.wait_ge(s("y"), b + 1)
                    if b:
                        dve.wait_ge(s("attn_added"), b)
                    dve.scalar_tensor_tensor(y_scaled, y, vec["L1_attn_gout"], PS[2][:], ALU.mult, ALU.mult).then_inc(s("y_scaled"), 1)
                    dve.wait_ge(s("y_scaled"), b + 1)
                    dve.wait_ge(s("mix_added"), b + 1)
                    dve.tensor_tensor(cols(xT, b), cols(xT, b), y_scaled, ALU.add).then_inc(s("attn_added"), 1)

                for i in range(-1, B + 1):
                    now, before, after = 0 <= i < B, i >= 1, i + 1 < B
                    if now:
                        qkv_bias(i, (0, 1))
                        mixes(i)
                        qkv_bias(i, (2, 3))
                    if after:
                        gate_rows(i + 1)
                    if now:
                        mean_squares(i)
                    if after:
                        add_rows(i + 1)
                    if now:
                        norm_qk(i)
                    if after:
                        centre(i + 1)
                    if now:
                        turn_parts(i)
                        rotate(i)
                    if before:
                        invert_y(i - 1)
                    if now:
                        mix_into_x(i)
                    if after:
                        invert_deviation(i + 1)
                    if now:
                        own_heads(i)
                    if after:
                        normalise(i + 1)
                    if before:
                        project_into_x(i - 1)
                    if now:
                        divide(i)

            def pool_prog(pool):
                def swapped_part(b):
                    if b == 0:
                        pool.wait_ge(s("prep"), 1 + 4 * TPB + 2)
                    pool.wait_ge(s("normed"), b + 1)
                    if b:
                        pool.wait_ge(s("rotated"), b)
                    swapped = normed.rearrange("p t (w two) -> p (t w) two", two=2)[:, :, ::-1]
                    pool.tensor_tensor(part_s.rearrange("p t (w two) -> p (t w) two", two=2), swapped,
                                       table_s.rearrange("p t (w two) -> p (t w) two", two=2), ALU.mult).then_inc(s("part_s"), 1)

                for t in range(TILES):
                    if t >= 2 * TPB and t % TPB == 0:
                        swapped_part(t // TPB - 2)
                    if t >= R:
                        pool.wait_ge(s("tile"), t - R + 1)
                    for k in range(K0):
                        pool.indirect_dma_start(out=got[:, t % R, k, :], out_offset=None, in_=Ys0,
                                                in_offset=bass.IndirectOffsetOnAxis(ap=place0[k][:, t:t + 1], axis=0)).then_inc(sem(f"got0_{t % R}"), 16)
                swapped_part(B - 2)
                swapped_part(B - 1)

            stage(pe_prog, act_prog, dve_prog, pool_prog)

        layer1()

        CH = 16
        toeplitz = arena[:, 8192:12288].rearrange("p (r c t) -> p r c t", r=2, c=CH)

        def load_toeplitz(sp, g):
            src = bass.AP(kernel_pad.tensor, g * CH * 2 * P, [[1, P], [2 * P, CH], [1, P]])
            sp.dma_start(toeplitz[:, g % 2, :, :], src).then_inc(sem(f"toeplitz{g % 2}"), 16)

        def layer2_loads(sp):
            load_toeplitz(sp, 0)
            load_toeplitz(sp, 1)
            sp.dma_start(arena[:, 0:4096].rearrange("p (e f) -> p e f", e=E2), A["L2_ffn_W1"].rearrange("e i f -> i e f")).then_inc(sem("experts2_in"), 16)
            sp.dma_start(arena[:, 4096:8192].rearrange("p (e c d) -> p e c d", e=E2, c=F2 // P),
                         A["L2_ffn_W2"].rearrange("e (c p) d -> p e c d", p=P)).then_inc(sem("experts2_in"), 16)

        layer_norm(2, True)
        logits2 = work[:, 4096:4096 + TILES * E2].rearrange("p (t e) -> p t e", e=E2)
        shifted2 = work[:, 4608:4608 + TILES * E2].rearrange("p (t e) -> p t e", e=E2)
        top8_2 = sb("top8_2", [P, TILES, 8])
        gate2 = sb("gate2", [P, TILES])

        def gate2_act(act, s):
            act.wait_ge(s("shifted"), 1)
            act.activation(shifted2, shifted2, ACT.Exp).then_inc(s("exp"), 1)

        def gate2_dve(dve, s):
            dve.tensor_tensor(shifted2, logits2, top8_2[:, :, 0:1].broadcast_to([P, TILES, E2]), ALU.subtract).then_inc(s("shifted"), 1)
            dve.wait_ge(s("exp"), 1)
            dve.tensor_reduce(gate2[:], shifted2, AX.X, ALU.add).then_inc(s("gate_sum"), 1)
            dve.wait_ge(s("gate_sum"), 1)
            dve.reciprocal(gate2[:], gate2[:]).then_inc(s("gate"), 1)

        place2, expert_row2 = routing(2, E2, 1, Wr2[:], rows["L2_ffn_br"][:], S2, Xs2, logits2, top8_2, gate2_act, 1,
                                      work[:, 1024:4096], gate2_dve)

        conv = arena[:, 12288:16384].rearrange("p (t d) -> p t d", d=D)
        NJ = TPB - 1

        def convolution():
            s = lambda n: sem(f"conv_{n}")
            state = work[:, 0:NJ * 1024].rearrange("p (j n) -> p j n", j=NJ)
            weighted = work[:, 3072:3072 + NJ * 1024].rearrange("p (j n) -> p j n", j=NJ)
            seq = lambda buf: buf.rearrange("p (b t) d -> p b t d", t=TPB)

            def sp_prog(sp):
                for g in range(2, D // CH):
                    sp.wait_ge(s("inside"), g - 1)
                    load_toeplitz(sp, g)
                sp.wait_ge(sem("experts2_in"), 32)

            inside = work[:, 6144:7168].rearrange("p (r n) -> p r n", r=2)
            NG = D // CH

            def pe_prog(pe):
                for j in range(NJ):
                    for h in range(2):
                        n = 2 * j + h
                        u = seq(xtok[:])[:, 4 * h:4 * h + 4, j, :]
                        m = pe.matmul(PS[n][:].rearrange("p (b d) -> p b d", d=D), into_state[:], u, start=True, stop=(j == 0))
                        if j:
                            pe.wait_ge(s("state"), n - 1)
                            m = pe.matmul(PS[n][:], turn_state[:], state[:, j - 1, h * 512:(h + 1) * 512], start=False, stop=True)
                        m.then_inc(s("states"), 1)

                def triangles(g):
                    pe.wait_ge(sem(f"toeplitz{g % 2}"), 16 * (g // 2 + 1))
                    if g >= 2:
                        pe.wait_ge(s("inside_sb"), g - 1)
                    for c in range(CH):
                        q, j = divmod(c, 4)
                        last = pe.matmul(PS[6 + g % 2][32 * j:32 * j + 32, q * P:(q + 1) * P], xtok[:, :, g * CH + c],
                                         toeplitz[:, g % 2, c, :], start=True, stop=True)
                    last.then_inc(s("inside"), 1)

                def turn_triangles(g):
                    pe.wait_ge(s("inside_sb"), g + 1)
                    pe.wait_ge(s("weighted"), 2)
                    if g >= 2:
                        pe.wait_ge(s("inside_out"), g - 1)
                    for q in range(4):
                        last = pe.transpose(PS[g % 2][:, q * P:(q + 1) * P], inside[:, g % 2, q * P:(q + 1) * P], ident)
                    last.then_inc(s("inside_turned"), 1)

                for g in range(NG + 1):
                    if g < NG:
                        triangles(g)
                    if g >= 1:
                        turn_triangles(g - 1)
                pe.wait_ge(s("weighted"), 2 * NJ)
                for j in range(NJ):
                    for h in range(2):
                        n = 2 * j + h
                        if n >= 2:
                            pe.wait_ge(s("joined"), n - 1)
                        pe.matmul(PS[4 + n % 2][:], from_state[:], weighted[:, j, h * 512:(h + 1) * 512], start=True, stop=True).then_inc(s("across"), 1)

            def act_prog(act):
                for n in range(2 * NJ):
                    j, h = divmod(n, 2)
                    act.wait_ge(s("states"), n + 1)
                    act.activation(state[:, j, h * 512:(h + 1) * 512], PS[n][:], ACT.Copy).then_inc(s("state"), 1)
                for g in range(NG):
                    act.wait_ge(s("inside"), g + 1)
                    if g >= 2:
                        act.wait_ge(s("inside_turned"), g - 1)
                    act.activation(inside[:, g % 2, :], PS[6 + g % 2][:], ACT.Copy).then_inc(s("inside_sb"), 1)

            def dve_prog(dve):
                for n in range(2 * NJ):
                    j, h = divmod(n, 2)
                    dve.wait_ge(s("state"), n + 1)
                    dve.tensor_tensor(weighted[:, j, h * 512:(h + 1) * 512].rearrange("p (b d) -> p b d", d=D),
                                      PS[n][:].rearrange("p (b d) -> p b d", d=D),
                                      to_taps[:].unsqueeze(1).broadcast_to([P, 4, D]), ALU.mult).then_inc(s("weighted"), 1)
                for g in range(NG):
                    dve.wait_ge(s("inside_turned"), g + 1)
                    dve.tensor_copy(conv[:, :, g * CH:(g + 1) * CH].rearrange("p t c -> p c t"),
                                    PS[g % 2][:].rearrange("p (c t) -> p c t", t=TILES)).then_inc(s("inside_out"), 1)
                dve.wait_ge(s("inside_out"), NG)
                for n in range(2 * NJ):
                    j, h = divmod(n, 2)
                    dve.wait_ge(s("across"), n + 1)
                    c = seq(conv)[:, 4 * h:4 * h + 4, j + 1, :]
                    dve.tensor_tensor(c, c, PS[4 + n % 2][:].rearrange("p (b d) -> p b d", d=D), ALU.add).then_inc(s("joined"), 1)
            stage(pe_prog, act_prog, dve_prog, sort_pool(2, 1, Xs2, place2), sp_prog)

        convolution()

        def gating():
            s = lambda n: sem(f"gating_{n}")
            ring2 = lambda i: work[:, i * 1024:(i + 1) * 1024].rearrange("p (r n) -> p r n", r=2)
            convT, left, right, product = (ring2(i) for i in range(4))
            backward = ident[:, ::-1]

            def pe_prog(pe):
                def head(b):
                    if b >= 2:
                        pe.wait_ge(s("convT"), b - 1)
                    for t in range(TPB):
                        last = pe.matmul(PS[b % 2][:, t * P:(t + 1) * P], conv[:, b * TPB + t, :], backward, start=True, stop=True)
                    last.then_inc(s("turned"), 1)
                    if b >= 2:
                        pe.wait_ge(s("right"), b - 1)
                    pe.matmul(PS[4 + b % 2][:], WT["gate"], cols(xn, b), start=True, stop=True).then_inc(s("gate"), 1)

                def mid(b):
                    pe.wait_ge(s("convT"), b + 1)
                    if b >= 2:
                        pe.wait_ge(s("left"), b - 1)
                    pe.matmul(PS[2 + b % 2][:], WT["ss"], convT[:, b % 2, :], start=True, stop=True).then_inc(s("ss"), 1)

                def tail(b):
                    pe.wait_ge(s("product"), b + 1)
                    if b >= 2:
                        pe.wait_ge(s("added"), b - 1)
                    pe.matmul(PS[6 + b % 2][:], WT["fin"], product[:, b % 2, :], start=True, stop=True).then_inc(s("fin"), 1)

                for i in range(B + 2):
                    if i < B:
                        head(i)
                    if 1 <= i <= B:
                        mid(i - 1)
                    if i >= 2:
                        tail(i - 2)

            def act_prog(act):
                for i in range(B + 1):
                    if i < B:
                        act.wait_ge(s("turned"), i + 1)
                        if i >= 2:
                            act.wait_ge(s("ss"), i - 1)
                        act.activation(convT[:, i % 2, :], PS[i % 2][:], ACT.Copy).then_inc(s("convT"), 1)
                    if i >= 1:
                        b = i - 1
                        act.wait_ge(s("gate"), b + 1)
                        if b >= 2:
                            act.wait_ge(s("product"), b - 1)
                        act.activation(right[:, b % 2, :], PS[4 + b % 2][:], ACT.Gelu, bias=vec["L2_attn_gate_b"]).then_inc(s("right"), 1)
                        act.wait_ge(s("ss"), b + 1)
                        act.activation(left[:, b % 2, :], PS[2 + b % 2][:], ACT.Gelu, bias=vec["L2_attn_ss_b"]).then_inc(s("left"), 1)

            def dve_prog(dve):
                for i in range(B + 1):
                    if i < B:
                        dve.wait_ge(s("left"), i + 1)
                        dve.wait_ge(s("right"), i + 1)
                        if i >= 2:
                            dve.wait_ge(s("fin"), i - 1)
                        dve.tensor_tensor(product[:, i % 2, :], left[:, i % 2, :], right[:, i % 2, :], ALU.mult).then_inc(s("product"), 1)
                    if i >= 1:
                        b = i - 1
                        dve.wait_ge(s("fin"), b + 1)
                        dve.scalar_tensor_tensor(cols(xT, b), PS[6 + b % 2][:], vec["L2_attn_fin_b"], cols(xT, b), ALU.add, ALU.add).then_inc(s("added"), 1)
            stage(pe_prog, act_prog, dve_prog)

        gating()
        experts(2, 1, S2, Xs2, Ys2, expert_row2, arena[:, 0:4096], WT["b1"], arena[:, 4096:8192], b2[:], 32)
        combine(2, 1, Ys2, place2, lambda t, k: gate2[:, t:t + 1])
        layer_norm(3, False)

        def scan():
            s = lambda n: sem(f"scan_{n}")
            HALF = B // 2
            lam = work[:, 0:2 * T].rearrange("p (r n) -> p r n", r=2)
            hs = work[:, 1024:1024 + 2 * T].rearrange("p (r n) -> p r n", r=2)
            y = work[:, 2048:2048 + 2 * T].rearrange("p (r n) -> p r n", r=2)

            def pe_prog(pe):
                for h in range(2):
                    for j in range(HALF):
                        lanes = slice(NL * j, NL * (j + 1))
                        pe.matmul(PS[h][lanes, :], WT["lam"], cols(xn, h * HALF + j), start=True, stop=True)
                        last = pe.matmul(PS[2 + h][lanes, :], WT["bu"], cols(xn, h * HALF + j), start=True, stop=True)
                    last.then_inc(s("inputs"), 1)
                for b in range(B):
                    h, j = divmod(b, HALF)
                    lanes = slice(NL * j, NL * (j + 1))
                    pe.wait_ge(s("states"), h + 1)
                    if b >= 4:
                        pe.wait_ge(s("y"), b - 3)
                    pe.matmul(PS[4 + b % 4][:], WT["c"][lanes, :], hs[lanes, h, :], start=True, stop=True).then_inc(s("read"), 1)

            def act_prog(act):
                for h in range(2):
                    act.wait_ge(s("inputs"), h + 1)
                    act.activation(lam[:, h, :], PS[h][:], ACT.Sigmoid, bias=bl4[:]).then_inc(s("lam"), 1)

            def dve_prog(dve):
                for h in range(2):
                    dve.wait_ge(s("lam"), h + 1)
                    dve.tensor_tensor_scan(hs[:, h, :], lam[:, h, :], PS[2 + h][:], 0.0, ALU.mult, ALU.add).then_inc(s("states"), 1)
                for b in range(B):
                    dve.wait_ge(s("read"), b + 1)
                    if b >= 2:
                        dve.wait_ge(s("added"), b - 1)
                    dve.scalar_tensor_tensor(y[:, b % 2, :], cols(xn, b), vec["L3_attn_Dp"], PS[4 + b % 4][:], ALU.mult, ALU.add).then_inc(s("y"), 1)
                    dve.wait_ge(s("y"), b + 1)
                    dve.tensor_tensor(cols(xT, b), cols(xT, b), y[:, b % 2, :], ALU.add).then_inc(s("added"), 1)
            stage(pe_prog, act_prog, dve_prog)

        scan()

        oT_all = arena[:, 0:N]
        SCALE = float(1.0 / np.sqrt(np.float32(HD)))
        HQ, HS, HV = 9, 7, 9

        def attention():
            s = lambda n: sem(f"att_{n}")
            ring = lambda a, n: arena[:, a:a + 2 * n].rearrange("p (r n) -> p r n", r=2)
            qk = ring(4096, H * H * HD).rearrange("p r (h g d) -> p r h g d", h=H, g=H)
            pv = ring(8192, H * H * HD).rearrange("p r (g h d) -> p r g h d", h=H, g=H)
            qkv, score, prob = ring(12288, 3 * D), ring(13056, H * H), ring(13568, H * H)
            weights, bias = arena[:, 14080:14464], arena[:, 14464:14848]
            inv = arena[:, 14848:14848 + TILES]
            top, den = arena[:, 14912:14912 + H], arena[:, 14944:14944 + H]
            sq = work[:, 0:1024].rearrange("p (r n) -> p r n", r=2)
            wdownT, bdown_all = work[0:LAT, 1024:1152], work[0:LAT, 1152:1280]
            heads = lambda t: t.rearrange("p (h d) -> p h d", d=HD)
            kv_heads = lambda t: t.rearrange("p (h two d) -> p two h d", two=2, d=HD)
            q_of = lambda n: heads(qkv[:, n % 2, 0:D])
            k_of = lambda n: heads(qkv[:, n % 2, D:2 * D])
            v_of = lambda n: heads(qkv[:, n % 2, 2 * D:3 * D])
            g3 = lambda t: t.rearrange("p (h g) -> p h g", g=H)

            def multiply_qk(eng, n, h0, h1):
                return eng.tensor_tensor(qk[:, n % 2, h0:h1], q_of(n)[:, h0:h1].unsqueeze(2).broadcast_to([P, h1 - h0, H, HD]),
                                         k_of(n).unsqueeze(1).broadcast_to([P, h1 - h0, H, HD]), ALU.mult)

            def multiply_pv(eng, n, h0, h1):
                return eng.tensor_tensor(pv[:, n % 2].rearrange("p g h d -> p h g d")[:, h0:h1],
                                         g3(prob[:, n % 2])[:, h0:h1].unsqueeze(3).broadcast_to([P, h1 - h0, H, HD]),
                                         v_of(n).unsqueeze(1).broadcast_to([P, h1 - h0, H, HD]), ALU.mult)

            def pe_prog(pe):
                pe.transpose(PS[0][0:LAT, 0:P], Wdown[:], ident).then_inc(s("wdown_turned"), 1)
                for b in range(B):
                    pe.wait_ge(s("sq"), b + 1)
                    for t in range(TPB):
                        last = pe.matmul(PS[1][:, b * TPB + t:b * TPB + t + 1], sq[:, b % 2, t * P:(t + 1) * P], ones_mean[:, 0:1],
                                         start=True, stop=True)
                    last.then_inc(s("ms"), 1)
                pe.wait_ge(s("wdownT"), 1)
                pe.matmul(PS[2][:, 0:2 * D], wdownT, Wup[:], start=True, stop=True).then_inc(s("kv_weights"), 1)
                pe.matmul(PS[3][:, 0:2 * D], bdown_all, Wup[:], start=True, stop=True).then_inc(s("kv_bias"), 1)
                pe.wait_ge(s("weights"), 1)

                def project(n):
                    if n >= 2:
                        pe.wait_ge(s("qkv"), n - 1)
                    pe.matmul(PS[n % 2][:, 0:3 * D], xn[:, n * P:(n + 1) * P], weights, start=True, stop=True).then_inc(s("projected"), 1)

                def sum_width(n):
                    pe.wait_ge(s("product"), n + 1)
                    pe.wait_ge(s("product_pool"), n + 1)
                    if n >= 2:
                        pe.wait_ge(s("scores"), n - 1)
                    for d in range(HD):
                        last = pe.matmul(PS[2 + n % 2][:, 0:(H - HS) * H], ident, qk[:, n % 2, HS:H, :, d].rearrange("p h g -> p (h g)"),
                                         start=(d == 0), stop=(d == HD - 1))
                    last.then_inc(s("width_summed"), 1)

                def sum_heads(n):
                    b, t = divmod(n, TPB)
                    pe.wait_ge(s("weighted"), n + 1)
                    pe.wait_ge(s("weighted_pool"), n + 1)
                    if t == 0 and b >= 2:
                        pe.wait_ge(s("oT"), b - 1)
                    for g in range(H):
                        last = pe.matmul(PS[4 + b % 2][:, t * P:(t + 1) * P], pv[:, n % 2, g].rearrange("p h d -> p (h d)"), ident,
                                         start=(g == 0), stop=(g == H - 1))
                    last.then_inc(s("heads_summed"), 1)

                project(0)
                for n in range(TILES + 2):
                    if n >= 2:
                        sum_heads(n - 2)
                    if n + 1 < TILES:
                        project(n + 1)
                    if n < TILES:
                        sum_width(n)

            def act_prog(act):
                for b in range(B):
                    if b >= 2:
                        act.wait_ge(s("ms"), b - 1)
                    act.activation(sq[:, b % 2, :], cols(xn, b), ACT.Square).then_inc(s("sq"), 1)
                act.wait_ge(s("ms"), B)
                act.activation(inv, PS[1][:, 0:TILES], ACT.Sqrt, bias=eps_r3[:]).then_inc(s("dev"), 1)
                for n in range(TILES + 1):
                    if n < TILES:
                        act.wait_ge(s("width_summed"), n + 1)
                        if n >= 2:
                            act.wait_ge(s("exp"), n - 1)
                        act.activation(score[:, n % 2, HS * H:], PS[2 + n % 2][:, 0:(H - HS) * H], ACT.Copy).then_inc(s("scores"), 1)
                        act.wait_ge(s("shifted"), n + 1)
                        if n >= 2:
                            act.wait_ge(s("weighted"), n - 1)
                            act.wait_ge(s("weighted_pool"), n - 1)
                        act.activation(prob[:, n % 2, :], score[:, n % 2, :], ACT.Exp, scale=SCALE).then_inc(s("exp"), 1)
                    if n % TPB == 2 and n > TPB:
                        gather(act, n // TPB - 1)
                gather(act, B - 1)

            def gather(act, b):
                act.wait_ge(s("heads_summed"), TPB * (b + 1))
                act.activation(cols(oT_all, b), PS[4 + b % 2][:], ACT.Copy).then_inc(s("oT"), 1)

            def dve_prog(dve):
                gamma = vec["L3_ffn_gamma1"]
                bq_row, bup_row = rows["L3_ffn_bq"], rows["L3_ffn_bup"]
                dve.tensor_copy(bdown_all, bdown[:].broadcast_to([LAT, P]))
                dve.wait_ge(s("wdown_turned"), 1)
                dve.tensor_copy(wdownT, PS[0][0:LAT, 0:P]).then_inc(s("wdownT"), 1)
                dve.tensor_scalar(weights[:, 0:D], Wq[:], gamma, None, ALU.mult)
                dve.tensor_copy(bias[:, 0:D], bq_row[:])
                dve.wait_ge(s("kv_weights"), 1)
                dve.wait_ge(s("kv_bias"), 1)
                for i in range(2):
                    part = slice((1 + i) * D, (2 + i) * D)
                    dve.tensor_scalar(heads(weights[:, part]), kv_heads(PS[2][:, 0:2 * D])[:, i], gamma, None, ALU.mult)
                    dve.tensor_tensor(heads(bias[:, part]), kv_heads(PS[3][:, 0:2 * D])[:, i], kv_heads(bup_row[:])[:, i], ALU.add)
                dve.wait_ge(s("dev"), 1)
                dve.reciprocal(inv, inv).then_inc(s("weights"), 1)
                dve.wait_ge(s("weights"), 1)

                def products(n):
                    dve.wait_ge(s("projected"), n + 1)
                    if n >= 2:
                        dve.wait_ge(s("weighted_pool"), n - 1)
                        dve.wait_ge(s("weighted"), n - 1)
                    dve.scalar_tensor_tensor(qkv[:, n % 2, :], PS[n % 2][:, 0:3 * D], inv[:, n:n + 1], bias, ALU.mult, ALU.add).then_inc(s("qkv"), 1)
                    dve.wait_ge(s("qkv"), n + 1)
                    if n >= 2:
                        dve.wait_ge(s("width_summed"), n - 1)
                        dve.wait_ge(s("half_summed"), n - 1)
                        dve.wait_ge(s("exp"), n - 1)
                    multiply_qk(dve, n, HS, HQ).then_inc(s("product"), 1)
                    multiply_qk(dve, n, 0, HS).then_inc(s("product_half"), 1)
                    dve.wait_ge(s("product_half"), n + 1)
                    dve.tensor_reduce(score[:, n % 2, 0:HS * H], qk[:, n % 2, 0:HS].rearrange("p h g d -> p (h g) d"), AX.X, ALU.add).then_inc(s("half_summed"), 1)

                def shift(n):
                    dve.wait_ge(s("half_summed"), n + 1)
                    dve.wait_ge(s("scores"), n + 1)
                    dve.tensor_reduce(top, g3(score[:, n % 2]), AX.X, ALU.max).then_inc(s("top"), 1)
                    dve.wait_ge(s("top"), n + 1)
                    dve.tensor_tensor(g3(score[:, n % 2]), g3(score[:, n % 2]), top.unsqueeze(2).broadcast_to([P, H, H]), ALU.subtract).then_inc(s("shifted"), 1)

                def weigh(n):
                    dve.wait_ge(s("exp"), n + 1)
                    dve.tensor_reduce(den, g3(prob[:, n % 2]), AX.X, ALU.add).then_inc(s("den"), 1)
                    dve.wait_ge(s("den"), 2 * n + 1)
                    dve.reciprocal(den, den).then_inc(s("den"), 1)
                    dve.wait_ge(s("den"), 2 * n + 2)
                    dve.tensor_tensor(g3(prob[:, n % 2]), g3(prob[:, n % 2]), den.unsqueeze(2).broadcast_to([P, H, H]), ALU.mult).then_inc(s("prob"), 1)
                    dve.wait_ge(s("prob"), n + 1)
                    if n >= 2:
                        dve.wait_ge(s("heads_summed"), n - 1)
                    multiply_pv(dve, n, 0, HV).then_inc(s("weighted"), 1)

                for n in range(TILES + 1):
                    if n >= 1:
                        shift(n - 1)
                    if n < TILES:
                        products(n)
                    if n >= 1:
                        weigh(n - 1)

            def pool_prog(pool):
                for n in range(TILES + 1):
                    if n < TILES:
                        pool.wait_ge(s("qkv"), n + 1)
                        if n >= 2:
                            pool.wait_ge(s("width_summed"), n - 1)
                        multiply_qk(pool, n, HQ, H).then_inc(s("product_pool"), 1)
                    if n >= 1:
                        pool.wait_ge(s("prob"), n)
                        if n >= 3:
                            pool.wait_ge(s("heads_summed"), n - 2)
                        multiply_pv(pool, n - 1, HV, H).then_inc(s("weighted_pool"), 1)
            stage(pe_prog, act_prog, dve_prog, pool_prog)

        attention()

        def post():
            s = lambda n: sem(f"post_{n}")
            off = [N]

            def take(n):
                off[0] += n
                return arena[:, off[0] - n:off[0]]
            two = lambda n=T: take(2 * n).rearrange("p (r n) -> p r n", r=2)
            sq, total = two(), two()
            logit, gate = two(TPB * E3), two(TPB * E3)
            inv, top, den = take(TPB), take(TPB), take(TPB)
            acc = take(TILES * D).rearrange("p (t d) -> p t d", d=D)
            experts = work[:, 0:E3 * D]
            gate_weights = work[:, E3 * D:E3 * D + E3]
            product = lambda b, pair, i, j: ((b * 2 + pair) * 2 + i) * 2 + j

            def pe_prog(pe):
                def project(b):
                    if b:
                        pe.wait_ge(s("x2"), b)
                    pe.matmul(PS[0][:], Wo[:], cols(oT_all, b), start=True, stop=True).then_inc(s("z"), 1)

                def gates(b):
                    pe.wait_ge(s("x2"), b + 1)
                    pe.wait_ge(s("sq"), b + 1)
                    if b == 0:
                        pe.wait_ge(s("weights"), 1)
                    if b >= 2:
                        pe.wait_ge(s("logit"), b - 1)
                    for t in range(TPB):
                        pe.matmul(PS[1 + b % 2][:, TPB * E3 + t:TPB * E3 + t + 1], sq[:, b % 2, t * P:(t + 1) * P], ones_mean[:, 0:1], start=True, stop=True)
                        last = pe.matmul(PS[1 + b % 2][:, t * E3:(t + 1) * E3], cols(xn, b)[:, t * P:(t + 1) * P], gate_weights, start=True, stop=True)
                    last.then_inc(s("logits"), 1)
                    pe.wait_ge(s("total"), b + 1)
                    if b:
                        pe.wait_ge(s("acc_begun"), b)
                    for t in range(TPB):
                        last = pe.transpose(PS[3][:, t * P:(t + 1) * P], total[:, b % 2, t * P:(t + 1) * P], ident)
                    last.then_inc(s("total_turned"), 1)

                def apply(b, pair, i):
                    for j in range(2):
                        n, t = product(b, pair, i, j), 2 * pair + j
                        if n >= 4:
                            pe.wait_ge(s("taken"), n - 3)
                        pe.matmul(PS[4 + n % 4][:], cols(xn, b)[:, t * P:(t + 1) * P], experts[:, 4 * D * i:4 * D * (i + 1)],
                                  start=True, stop=True).then_inc(s("applied"), 1)

                project(0)
                gates(0)
                for b in range(B):
                    apply(b, 0, 0)
                    apply(b, 0, 1)
                    if b + 1 < B:
                        project(b + 1)
                    apply(b, 1, 0)
                    if b + 1 < B:
                        gates(b + 1)
                    apply(b, 1, 1)

            def act_prog(act):
                def begin(b):
                    act.wait_ge(s("total_turned"), b + 1)
                    act.activation(acc[:, b * TPB:(b + 1) * TPB, :], PS[3][:].rearrange("p (t d) -> p t d", d=D), ACT.Copy).then_inc(s("acc_begun"), 1)

                for b in range(B):
                    act.wait_ge(s("x2"), b + 1)
                    if b >= 2:
                        act.wait_ge(s("logits"), b - 1)
                    act.activation(sq[:, b % 2, :], cols(xn, b), ACT.Square).then_inc(s("sq"), 1)
                    act.wait_ge(s("logits"), b + 1)
                    act.wait_ge(s("inv_free"), b + 1)
                    act.activation(inv, PS[1 + b % 2][:, TPB * E3:TPB * E3 + TPB], ACT.Sqrt, bias=eps_r3[:]).then_inc(s("dev"), 1)
                    begin(b)
                    act.wait_ge(s("shifted"), b + 1)
                    if b >= 2:
                        act.wait_ge(s("acc"), TPB * (b - 1))
                    act.activation(gate[:, b % 2, :], logit[:, b % 2, :], ACT.Exp).then_inc(s("exp"), 1)

            def dve_prog(dve):
                g3 = lambda buf, b: buf[:, b % 2, :].rearrange("p (t e) -> p t e", e=E3)
                gamma = vec["L3_ffn_gamma2"]
                dve.sem_inc(s("inv_free"), 1)
                dve.tensor_scalar(experts, We[:].rearrange("p e d -> p (e d)"), gamma, None, ALU.mult)
                dve.tensor_scalar(gate_weights, Wg[:], gamma, None, ALU.mult).then_inc(s("weights"), 1)

                def front(b):
                    dve.wait_ge(s("z"), b + 1)
                    dve.scalar_tensor_tensor(cols(xn, b), PS[0][:], vec["L3_ffn_bo"], cols(xn, b), ALU.add, ALU.add).then_inc(s("x2"), 1)
                    dve.wait_ge(s("x2"), b + 1)
                    if b >= 2:
                        dve.wait_ge(s("total_turned"), b - 1)
                    dve.tensor_tensor(total[:, b % 2, :], cols(xT, b), cols(xn, b), ALU.add).then_inc(s("total"), 1)

                def gate_logits(b):
                    dve.wait_ge(s("dev"), b + 1)
                    dve.reciprocal(inv, inv).then_inc(s("inv"), 1)
                    dve.wait_ge(s("inv"), b + 1)
                    if b >= 2:
                        dve.wait_ge(s("exp"), b - 1)
                    spread = lambda t: t.unsqueeze(2).broadcast_to([P, TPB, E3])
                    dve.tensor_tensor(g3(logit, b), PS[1 + b % 2][:, 0:TPB * E3].rearrange("p (t e) -> p t e", e=E3), spread(inv), ALU.mult).then_inc(s("logit"), 1)
                    dve.wait_ge(s("logit"), b + 1)
                    dve.tensor_tensor(g3(logit, b), g3(logit, b), rows["L3_ffn_bg"][:].unsqueeze(1).broadcast_to([P, TPB, E3]), ALU.add).then_inc(s("biased"), 1)
                    dve.wait_ge(s("biased"), b + 1)
                    dve.tensor_reduce(top, g3(logit, b), AX.X, ALU.max).then_inc(s("top"), 1)
                    dve.wait_ge(s("top"), b + 1)
                    dve.tensor_tensor(g3(logit, b), g3(logit, b), spread(top), ALU.subtract).then_inc(s("shifted"), 1)

                def back(b):
                    spread = lambda t: t.unsqueeze(2).broadcast_to([P, TPB, E3])
                    dve.wait_ge(s("exp"), b + 1)
                    dve.tensor_reduce(den, g3(gate, b), AX.X, ALU.add).then_inc(s("den"), 1)
                    dve.wait_ge(s("den"), 3 * b + 1)
                    dve.reciprocal(den, den).then_inc(s("den"), 1)
                    dve.wait_ge(s("den"), 3 * b + 2)
                    dve.tensor_tensor(den, den, inv, ALU.mult).then_inc(s("den"), 1)
                    dve.wait_ge(s("den"), 3 * b + 3)
                    dve.sem_inc(s("inv_free"), 1)
                    dve.tensor_tensor(g3(gate, b), g3(gate, b), spread(den), ALU.mult).then_inc(s("gate"), 1)

                front(0)
                gate_logits(0)
                back(0)
                for b in range(B):
                    dve.wait_ge(s("gate"), b + 1)
                    dve.wait_ge(s("acc_begun"), b + 1)
                    for pair in range(2):
                        for e in range(E3):
                            for j in range(2):
                                t, m = 2 * pair + j, product(b, pair, e // 4, j)
                                n = b * TPB + t
                                if e % 4 == 0:
                                    dve.wait_ge(s("applied"), m + 1)
                                if e:
                                    dve.wait_ge(s("sum"), (b * 2 + pair) * 2 * E3 + 2 * (e - 1) + j + 1)
                                dve.scalar_tensor_tensor(acc[:, n, :], PS[4 + m % 4][:, (e % 4) * D:(e % 4 + 1) * D],
                                                         gate[:, b % 2, t * E3 + e:t * E3 + e + 1], acc[:, n, :], ALU.mult, ALU.add).then_inc(s("sum"), 1)
                            if e % 4 == 3:
                                dve.wait_ge(s("sum"), (b * 2 + pair) * 2 * E3 + 2 * e + 2)
                                dve.sem_inc(s("taken"), 2)
                        dve.sem_inc(s("acc"), 2)
                        if pair == 0 and b + 1 < B:
                            front(b + 1)
                        if pair == 1 and b + 1 < B:
                            gate_logits(b + 1)
                            back(b + 1)

            def sp_prog(sp):
                for b in range(B):
                    sp.wait_ge(s("acc"), TPB * (b + 1))
                    sp.dma_start(out[b].rearrange("(t p) d -> p t d", p=P), acc[:, b * TPB:(b + 1) * TPB, :]).then_inc(s("out_stored"), 16)
                sp.wait_ge(s("out_stored"), 16 * B)
            stage(pe_prog, act_prog, dve_prog, None, sp_prog)

        post()
        def out_pe(pe):
            for b in range(B):
                if b >= 2:
                    pe.wait_ge(sem("out_copied"), b - 1)
                for t in range(TPB):
                    last = pe.transpose(PS[b % 2][:, t * P:(t + 1) * P], xT[:, b * T + t * P:b * T + (t + 1) * P], ident)
                last.then_inc(sem("out_turned"), 1)

        def out_act(act):
            for b in range(B):
                act.wait_ge(sem("out_turned"), b + 1)
                act.activation(xtok[:, b * TPB:(b + 1) * TPB, :], PS[b % 2][:].rearrange("p (t d) -> p t d", d=D), ACT.Copy).then_inc(sem("out_copied"), 1)

        def out_sp(sp):
            for b in range(B):
                sp.wait_ge(sem("out_copied"), b + 1)
                sp.dma_start(out[b].rearrange("(t p) d -> p t d", p=P), xtok[:, b * TPB:(b + 1) * TPB, :]).then_inc(sem("out_stored"), 16)
            sp.wait_ge(sem("out_stored"), 16 * B)

        final = (out_pe, out_act, None, None, out_sp)
        todo = stages if upto >= len(stages) else stages[:upto] + [final]

        block = ctx.enter_context(nc.Block())

        numbers = range(of_stage[0].num, of_stage[-1].num + 1)
        assert len(numbers) == len(of_stage)

        def run(eng, which):
            for n, st in enumerate(todo):
                current[0] = n
                if st[which] is not None:
                    st[which](eng)
                if n < len(todo) - 1:
                    eng.drain().then_inc(lasting["stage_done"], 1)
                    if which == 4:
                        eng.wait_ge(lasting["stage_done"], 5 * (n + 1))
                        eng.sem_clear(numbers)
                        eng.sem_inc(lasting["stage_go"], 1)
                    eng.wait_ge(lasting["stage_go"], n + 1)
                    eng.drain()

        @block.tensor
        def _(pe):
            run(pe, 0)

        @block.scalar
        def _(act):
            run(act, 1)

        @block.vector
        def _(dve):
            run(dve, 2)

        @block.gpsimd
        def _(pool):
            run(pool, 3)

        @block.sync
        def _(sp):
            run(sp, 4)


_OUT = ((B, T, D), "float32")


def kernel(**inputs):
    import concourse.bacc as bacc
    from concourse.bass_utils import run_bass_kernel_spmd

    nc = bacc.Bacc("TRN2", target_bir_lowering=False, num_devices=1)
    arrays, A = {}, {}
    for name, a in inputs.items():
        a = np.ascontiguousarray(a)
        arrays[name] = a
        A[name] = nc.dram_tensor(name, a.shape, mybir.dt.from_np(a.dtype), kind="ExternalInput").ap()
    packed, at = constants()
    arrays["constants"] = packed
    cst = nc.dram_tensor("constants", packed.shape, FP32, kind="ExternalInput").ap()
    out = nc.dram_tensor("out", _OUT[0], FP32, kind="ExternalOutput").ap()
    program(nc, A, cst, at, out)
    r = run_bass_kernel_spmd(nc, [arrays], core_ids=[0])
    return r.results[0]["out"]
```
